# Optimizing a Trainium2 kernel written in Bass

```python
import numpy as np
import jax
import jax.numpy as jnp

def _softmax(x, axis=-1):
    return jax.nn.softmax(x, axis=axis)

def _gelu(x):
    return jax.nn.gelu(x, approximate=True)

def _silu(x):
    return jax.nn.silu(x)

def _sigmoid(x):
    return jax.nn.sigmoid(x)

def _layernorm(x, axis=-1, eps=1e-05):
    m = jnp.mean(x, axis=axis, keepdims=True)
    v = jnp.var(x, axis=axis, keepdims=True)
    return (x - m) / jnp.sqrt(v + eps)

def _scatter_add(tgt, idx, src, axis=0):
    return tgt.at[idx].add(src)

def _segment_sum(src, seg, n):
    return jax.ops.segment_sum(src, seg, n)
kernel_name = 'mk_sandwich_d2_jaxref_r8_96122e'

def setup_inputs(seed: int=0):
    np.random.seed(seed)
    _w = jnp.asarray

    def _L0_attn_setup():
        import jax, jax.numpy as jnp
        import numpy as np
        D_INNER = 128
        STATE = 16
        DT_RANK = 64

        def _combine(carry, nxt):
            a1, b1 = carry
            a2, b2 = nxt
            return (a1 * a2, a2 * b1 + b2)
        key = jax.random.key(seed)
        k_u, k_x, k_dt, k_b = jax.random.split(key, 4)
        u = jax.random.normal(k_u, (2, 256, D_INNER), dtype=jnp.float32)
        A_log = jnp.broadcast_to(jnp.log(jnp.arange(1, STATE + 1, dtype=jnp.float32))[None, :], (D_INNER, STATE))
        W_x = jax.random.normal(k_x, (DT_RANK + 2 * STATE, D_INNER), dtype=jnp.float32) * 0.02
        W_dt = jax.random.normal(k_dt, (D_INNER, DT_RANK), dtype=jnp.float32) * 0.02
        dt_init = jnp.exp(jax.random.uniform(k_b, (D_INNER,), dtype=jnp.float32) * (np.log(0.1) - np.log(0.001)) + np.log(0.001))
        b_dt = dt_init + jnp.log(-jnp.expm1(-dt_init))
        D_param = jnp.ones((D_INNER,), dtype=jnp.float32)
        return {'u': u, 'A_log': A_log, 'W_x': W_x, 'W_dt': W_dt, 'b_dt': b_dt, 'D_param': D_param}
    _L0_attn_in = _L0_attn_setup()

    def _L0_ffn_setup():
        import jax, jax.numpy as jnp
        import numpy as np
        K = 2
        key = jax.random.key(seed)
        ks = jax.random.split(key, 6)
        B, S, D, U, E = (2, 256, 128, 512, 8)
        return {'x': jax.random.normal(ks[0], (B, S, D), dtype=jnp.float32), 'w_router': jax.random.normal(ks[1], (E, D), dtype=jnp.float32), 'w_up': jax.random.normal(ks[2], (E, U, D), dtype=jnp.float32), 'b_up': jax.random.normal(ks[3], (E, U), dtype=jnp.float32), 'w_down': jax.random.normal(ks[4], (E, D, U), dtype=jnp.float32), 'b_down': jax.random.normal(ks[5], (E, D), dtype=jnp.float32)}
    _L0_ffn_in = _L0_ffn_setup()

    def _L1_attn_setup():
        import jax, jax.numpy as jnp
        import numpy as np
        N_IN = 128
        KSIZE = 31
        PAD_L = 30
        HEADS = 16
        key = jax.random.key(seed)
        k1, k2 = jax.random.split(key)
        B, T, C = (2, 256, N_IN)
        x = jax.random.normal(k1, (B, T, C), dtype=jnp.float32)
        w_lin = jax.random.normal(k2, (HEADS * KSIZE, C), dtype=jnp.float32) * (1.0 / np.sqrt(C))
        return {'x': x, 'w_lin': w_lin}
    _L1_attn_in = _L1_attn_setup()

    def _L1_ffn_setup():
        import jax, jax.numpy as jnp
        import numpy as np
        DIM = 128
        DEPTH = 6
        HEADS = 16
        DIM_HEAD = 64
        WINDOW = 32
        INNER = HEADS * DIM_HEAD
        DIM_INNER = int(DIM * 4 * 2 / 3)
        QK_SCALE = 8.0

        def shift_tokens(t):
            a, s = jnp.split(t, 2, -1)
            s = jnp.pad(s, ((0, 0), (1, 0), (0, 0)))[:, :-1]
            return jnp.concatenate([a, s], -1)

        def l2norm(t):
            return t / jnp.maximum(jnp.linalg.norm(t, axis=-1, keepdims=True), 1e-12)

        def rotate_half(x):
            x1, x2 = jnp.split(x, 2, -1)
            return jnp.concatenate([-x2, x1], -1)

        def rotary_tables(n):
            half = jnp.arange(0, DIM_HEAD, 2, dtype=jnp.float32)
            inv_freq = 1.0 / 10000.0 ** (half / DIM_HEAD)
            t = jnp.arange(n, dtype=jnp.float32)
            freqs = t[:, None] * inv_freq[None, :]
            freqs = jnp.concatenate([freqs, freqs], -1)
            base_scale = (half + 0.4 * DIM_HEAD) / (1.4 * DIM_HEAD)
            power = (t - n // 2) / (WINDOW // 2)
            scale = base_scale[None, :] ** power[:, None]
            scale = jnp.concatenate([scale, scale], -1)
            return (freqs, scale)

        def local_attention(q, k, v):
            b, h, n, d = q.shape
            w = WINDOW
            nw = n // w
            bq = q.reshape(b, h, nw, w, d)
            bk = k.reshape(b, h, nw, w, d)
            bv = v.reshape(b, h, nw, w, d)

            def look(t):
                p = jnp.pad(t, ((0, 0), (0, 0), (1, 0), (0, 0), (0, 0)))
                return jnp.concatenate([p[:, :, :nw], p[:, :, 1:]], axis=3)
            bk2, bv2 = (look(bk), look(bv))
            seq = jnp.arange(n).reshape(nw, w)
            seq_p = jnp.pad(seq, ((1, 0), (0, 0)), constant_values=-1)
            jt = jnp.concatenate([seq_p[:nw], seq_p[1:]], axis=1)
            it = seq[:, :, None]
            jb = jt[:, None, :]
            mask = (it < jb) | (it > jb + w) | (jb == -1)
            sim = jnp.einsum('bhwie,bhwje->bhwij', bq, bk2) * QK_SCALE
            sim = jnp.where(mask, -jnp.finfo(sim.dtype).max, sim)
            attn = jax.nn.softmax(sim, -1)
            out = jnp.einsum('bhwij,bhwje->bhwie', attn, bv2)
            return out.reshape(b, h, n, d)

        def attn_layer(x, Wqkv, qs, ksc, Wo):
            b, n, _ = x.shape
            qkv = x @ Wqkv
            q, k, v = jnp.split(qkv, 3, -1)
            sh = lambda t: t.reshape(b, n, HEADS, DIM_HEAD).transpose(0, 2, 1, 3)
            q, k, v = (sh(q), sh(k), sh(v))
            q = l2norm(q) * qs
            k = l2norm(k) * ksc
            freqs, scale = rotary_tables(n)
            cos, sin = (jnp.cos(freqs), jnp.sin(freqs))
            q = q * cos * scale + rotate_half(q) * sin * scale
            inv = 1.0 / scale
            k = k * cos * inv + rotate_half(k) * sin * inv
            out = local_attention(q, k, v)
            out = out.transpose(0, 2, 1, 3).reshape(b, n, INNER)
            return out @ Wo

        def ffn_layer(x, g, bln, W1, b1, W2, b2):
            mu = x.mean(-1, keepdims=True)
            var = ((x - mu) ** 2).mean(-1, keepdims=True)
            xn = (x - mu) / jnp.sqrt(var + 1e-05) * g + bln
            hg = xn @ W1 + b1
            a, gate = jnp.split(hg, 2, -1)
            return a * jax.nn.gelu(gate, approximate=False) @ W2 + b2
        key = jax.random.key(seed)
        ks = jax.random.split(key, 8)
        B, N = (2, 256)
        init = lambda k, shape: jax.random.normal(k, shape, jnp.float32) * 0.02
        return {'x': jax.random.normal(ks[0], (B, N, DIM), jnp.float32), 'Wqkv': init(ks[1], (DEPTH, DIM, 3 * INNER)), 'q_scale': jnp.ones((DEPTH, DIM_HEAD), jnp.float32), 'k_scale': jnp.ones((DEPTH, DIM_HEAD), jnp.float32), 'Wo': init(ks[2], (DEPTH, INNER, DIM)), 'ln_g': jnp.ones((DEPTH, DIM), jnp.float32), 'ln_b': jnp.zeros((DEPTH, DIM), jnp.float32), 'W1': init(ks[3], (DEPTH, DIM, 2 * DIM_INNER)), 'b1': jnp.zeros((DEPTH, 2 * DIM_INNER), jnp.float32), 'W2': init(ks[4], (DEPTH, DIM_INNER, DIM)), 'b2': jnp.zeros((DEPTH, DIM), jnp.float32)}
    _L1_ffn_in = _L1_ffn_setup()
    _d = {'L0_attn_u': _L0_attn_in['u'], 'L0_attn_A_log': _L0_attn_in['A_log'], 'L0_attn_W_x': _L0_attn_in['W_x'], 'L0_attn_W_dt': _L0_attn_in['W_dt'], 'L0_attn_b_dt': _L0_attn_in['b_dt'], 'L0_attn_D_param': _L0_attn_in['D_param'], 'L0_ffn_w_router': _L0_ffn_in['w_router'], 'L0_ffn_w_up': _L0_ffn_in['w_up'], 'L0_ffn_b_up': _L0_ffn_in['b_up'], 'L0_ffn_w_down': _L0_ffn_in['w_down'], 'L0_ffn_b_down': _L0_ffn_in['b_down'], 'L1_attn_w_lin': _L1_attn_in['w_lin'], 'L1_ffn_Wqkv': _L1_ffn_in['Wqkv'], 'L1_ffn_q_scale': _L1_ffn_in['q_scale'], 'L1_ffn_k_scale': _L1_ffn_in['k_scale'], 'L1_ffn_Wo': _L1_ffn_in['Wo'], 'L1_ffn_ln_g': _L1_ffn_in['ln_g'], 'L1_ffn_ln_b': _L1_ffn_in['ln_b'], 'L1_ffn_W1': _L1_ffn_in['W1'], 'L1_ffn_b1': _L1_ffn_in['b1'], 'L1_ffn_W2': _L1_ffn_in['W2'], 'L1_ffn_b2': _L1_ffn_in['b2']}
    _x0 = _d['L0_attn_u']
    _d['L0_attn_u'] = jax.random.normal(jax.random.fold_in(jax.random.key(seed), 1), (4, 1024, 128), dtype=_x0.dtype)
    del _x0
    return _d

def reference(L0_attn_u, L0_attn_A_log, L0_attn_W_x, L0_attn_W_dt, L0_attn_b_dt, L0_attn_D_param, L0_ffn_w_router, L0_ffn_w_up, L0_ffn_b_up, L0_ffn_w_down, L0_ffn_b_down, L1_attn_w_lin, L1_ffn_Wqkv, L1_ffn_q_scale, L1_ffn_k_scale, L1_ffn_Wo, L1_ffn_ln_g, L1_ffn_ln_b, L1_ffn_W1, L1_ffn_b1, L1_ffn_W2, L1_ffn_b2):

    def _L0_attn_ref(u, A_log, W_x, W_dt, b_dt, D_param):
        import jax, jax.numpy as jnp
        import numpy as np
        D_INNER = 128
        STATE = 16
        DT_RANK = 64

        def _combine(carry, nxt):
            a1, b1 = carry
            a2, b2 = nxt
            return (a1 * a2, a2 * b1 + b2)
        N = A_log.shape[1]
        dt_rank = W_dt.shape[1]
        x_dbl = jnp.einsum('bld,ed->ble', u, W_x)
        dt_raw = x_dbl[..., :dt_rank]
        B_sel = x_dbl[..., dt_rank:dt_rank + N]
        C_sel = x_dbl[..., dt_rank + N:]
        dt = jax.nn.softplus(jnp.einsum('blr,dr->bld', dt_raw, W_dt) + b_dt)
        A = -jnp.exp(A_log)
        A_bar = jnp.exp(dt[..., None] * A)
        dB_u = (dt * u)[..., None] * B_sel[:, :, None, :]
        _, h = jax.lax.associative_scan(_combine, (A_bar, dB_u), axis=1)
        y = jnp.einsum('bldn,bln->bld', h, C_sel)
        return y + u * D_param

    def _L0_ffn_ref(x, w_router, w_up, b_up, w_down, b_down):
        import jax, jax.numpy as jnp
        import numpy as np
        K = 2
        logits = jnp.einsum('bsd,ed->bse', x, w_router)
        top_logits, idx = jax.lax.top_k(logits, K)
        router_weights = jax.nn.softmax(top_logits, axis=-1)
        h = jnp.einsum('eud,bsd->bseu', w_up, x) + b_up[None, None]
        h = jax.nn.gelu(h, approximate=False)
        y = jnp.einsum('edu,bseu->bsed', w_down, h) + b_down[None, None]
        y_k = jnp.take_along_axis(y, idx[..., None], axis=2)
        out = jnp.einsum('bskd,bsk->bsd', y_k, router_weights)
        return out

    def _L1_attn_ref(x, w_lin):
        import jax, jax.numpy as jnp
        import numpy as np
        N_IN = 128
        KSIZE = 31
        PAD_L = 30
        HEADS = 16
        B, T, C = x.shape
        H, K, P = (HEADS, KSIZE, PAD_L)
        R = C // H
        w = jnp.einsum('btc,fc->btf', x, w_lin).reshape(B, T, H, K)
        w = jax.nn.softmax(w.astype(jnp.float32), axis=-1).astype(x.dtype)
        w = w.transpose(0, 2, 1, 3)
        t_idx = jnp.arange(T)[:, None]
        s_idx = jnp.arange(T)[None, :]
        kidx = s_idx - t_idx + P
        mask = (kidx >= 0) & (kidx < K)
        kidx_c = jnp.clip(kidx, 0, K - 1)
        we = jnp.take_along_axis(w, jnp.broadcast_to(kidx_c, (B, H, T, T)), axis=-1)
        we = jnp.where(mask, we, jnp.zeros((), dtype=we.dtype))
        xh = x.reshape(B, T, H, R).transpose(0, 2, 1, 3)
        out = jnp.einsum('bhts,bhsr->bhtr', we, xh)
        return out.transpose(0, 2, 1, 3).reshape(B, T, C)

    def _L1_ffn_ref(x, Wqkv, q_scale, k_scale, Wo, ln_g, ln_b, W1, b1, W2, b2):
        import jax, jax.numpy as jnp
        import numpy as np
        DIM = 128
        DEPTH = 6
        HEADS = 16
        DIM_HEAD = 64
        WINDOW = 32
        INNER = HEADS * DIM_HEAD
        DIM_INNER = int(DIM * 4 * 2 / 3)
        QK_SCALE = 8.0

        def shift_tokens(t):
            a, s = jnp.split(t, 2, -1)
            s = jnp.pad(s, ((0, 0), (1, 0), (0, 0)))[:, :-1]
            return jnp.concatenate([a, s], -1)

        def l2norm(t):
            return t / jnp.maximum(jnp.linalg.norm(t, axis=-1, keepdims=True), 1e-12)

        def rotate_half(x):
            x1, x2 = jnp.split(x, 2, -1)
            return jnp.concatenate([-x2, x1], -1)

        def rotary_tables(n):
            half = jnp.arange(0, DIM_HEAD, 2, dtype=jnp.float32)
            inv_freq = 1.0 / 10000.0 ** (half / DIM_HEAD)
            t = jnp.arange(n, dtype=jnp.float32)
            freqs = t[:, None] * inv_freq[None, :]
            freqs = jnp.concatenate([freqs, freqs], -1)
            base_scale = (half + 0.4 * DIM_HEAD) / (1.4 * DIM_HEAD)
            power = (t - n // 2) / (WINDOW // 2)
            scale = base_scale[None, :] ** power[:, None]
            scale = jnp.concatenate([scale, scale], -1)
            return (freqs, scale)

        def local_attention(q, k, v):
            b, h, n, d = q.shape
            w = WINDOW
            nw = n // w
            bq = q.reshape(b, h, nw, w, d)
            bk = k.reshape(b, h, nw, w, d)
            bv = v.reshape(b, h, nw, w, d)

            def look(t):
                p = jnp.pad(t, ((0, 0), (0, 0), (1, 0), (0, 0), (0, 0)))
                return jnp.concatenate([p[:, :, :nw], p[:, :, 1:]], axis=3)
            bk2, bv2 = (look(bk), look(bv))
            seq = jnp.arange(n).reshape(nw, w)
            seq_p = jnp.pad(seq, ((1, 0), (0, 0)), constant_values=-1)
            jt = jnp.concatenate([seq_p[:nw], seq_p[1:]], axis=1)
            it = seq[:, :, None]
            jb = jt[:, None, :]
            mask = (it < jb) | (it > jb + w) | (jb == -1)
            sim = jnp.einsum('bhwie,bhwje->bhwij', bq, bk2) * QK_SCALE
            sim = jnp.where(mask, -jnp.finfo(sim.dtype).max, sim)
            attn = jax.nn.softmax(sim, -1)
            out = jnp.einsum('bhwij,bhwje->bhwie', attn, bv2)
            return out.reshape(b, h, n, d)

        def attn_layer(x, Wqkv, qs, ksc, Wo):
            b, n, _ = x.shape
            qkv = x @ Wqkv
            q, k, v = jnp.split(qkv, 3, -1)
            sh = lambda t: t.reshape(b, n, HEADS, DIM_HEAD).transpose(0, 2, 1, 3)
            q, k, v = (sh(q), sh(k), sh(v))
            q = l2norm(q) * qs
            k = l2norm(k) * ksc
            freqs, scale = rotary_tables(n)
            cos, sin = (jnp.cos(freqs), jnp.sin(freqs))
            q = q * cos * scale + rotate_half(q) * sin * scale
            inv = 1.0 / scale
            k = k * cos * inv + rotate_half(k) * sin * inv
            out = local_attention(q, k, v)
            out = out.transpose(0, 2, 1, 3).reshape(b, n, INNER)
            return out @ Wo

        def ffn_layer(x, g, bln, W1, b1, W2, b2):
            mu = x.mean(-1, keepdims=True)
            var = ((x - mu) ** 2).mean(-1, keepdims=True)
            xn = (x - mu) / jnp.sqrt(var + 1e-05) * g + bln
            hg = xn @ W1 + b1
            a, gate = jnp.split(hg, 2, -1)
            return a * jax.nn.gelu(gate, approximate=False) @ W2 + b2
        for i in range(DEPTH):
            x = attn_layer(shift_tokens(x), Wqkv[i], q_scale[i], k_scale[i], Wo[i]) + x
            x = ffn_layer(shift_tokens(x), ln_g[i], ln_b[i], W1[i], b1[i], W2[i], b2[i]) + x
        return x
    x = L0_attn_u
    x = x + _layernorm(_L0_attn_ref(_layernorm(x, axis=-1), L0_attn_A_log, L0_attn_W_x, L0_attn_W_dt, L0_attn_b_dt, L0_attn_D_param), axis=-1)
    x = x + _layernorm(_L0_ffn_ref(_layernorm(x, axis=-1), L0_ffn_w_router, L0_ffn_w_up, L0_ffn_b_up, L0_ffn_w_down, L0_ffn_b_down), axis=-1)
    x = x + _layernorm(_L1_attn_ref(_layernorm(x, axis=-1), L1_attn_w_lin), axis=-1)
    x = x + _layernorm(_L1_ffn_ref(_layernorm(x, axis=-1), L1_ffn_Wqkv, L1_ffn_q_scale, L1_ffn_k_scale, L1_ffn_Wo, L1_ffn_ln_g, L1_ffn_ln_b, L1_ffn_W1, L1_ffn_b1, L1_ffn_W2, L1_ffn_b2), axis=-1)
    return x

_drawn_inputs = setup_inputs


def setup_inputs(seed=0):
    import zlib

    import numpy as np

    out = dict(_drawn_inputs(seed))
    spreads = {'L0_attn_D_param': (1.0, 0.2),
     'L1_ffn_q_scale': (1.0, 0.6),
     'L1_ffn_k_scale': (1.0, 0.6),
     'L1_ffn_ln_g': (1.0, 0.6),
     'L1_ffn_ln_b': (0.0, 0.8),
     'L1_ffn_b1': (0.0, 0.8),
     'L1_ffn_b2': (0.0, 0.1)}
    factors = {'L0_attn_A_log': 7.561,
     'L0_attn_W_x': 5.271,
     'L0_attn_W_dt': 8.0,
     'L0_attn_b_dt': 7.172,
     'L0_ffn_b_down': 8.0,
     'L1_ffn_W1': 6.7,
     'L1_ffn_W2': 6.543}
    for name, (base, spread) in spreads.items():
        noise = np.random.default_rng([zlib.crc32(name.encode()), seed]).standard_normal(out[name].shape)
        drawn = base * np.exp(spread * noise) if base else spread * noise
        out[name] = jnp.asarray(drawn.astype(out[name].dtype))
    for name, factor in factors.items():
        out[name] = (out[name] * factor).astype(out[name].dtype)
    return out
```

```python
from contextlib import ExitStack

import concourse.bass as bass
from concourse import mybir
from concourse.alu_op_type import AluOpType as ALU

F32 = mybir.dt.float32
BF16 = mybir.dt.bfloat16
U16 = mybir.dt.uint16
ACT = mybir.ActivationFunctionType
AX = mybir.AxisListType.X

P = 128
D = 128
NSEQ, SLEN = 4, 1024
T = NSEQ * SLEN
PAD = 36
SEQW = PAD + SLEN
XW = NSEQ * SEQW
CH = 512
NCH = T // CH
CPS = SLEN // CH
EPS = 1e-5

MASKED = -1e37
BLK = 128
NBLK = T // BLK
BPS = SLEN // BLK
WIN = 32
HEADS, DH = 16, 64
HP = HEADS // 2
DEPTH = 6
INNER = HEADS * DH
FI = 341
FIT = [(0, P), (P, P), (2 * P, FI - 2 * P)]


def blk_off(n):
    return n * BLK + (n // BPS) * PAD + PAD


def chunk_off(c):
    return c * CH + (c // CPS) * PAD + PAD


class Chain:

    def __init__(self, eng, sem, base):
        self.eng, self.sem, self.count = eng, sem, base

    def link(self, ins):
        self.count = self.count + 1
        ins.then_inc(self.sem, 1)
        self.eng.wait_ge(self.sem, self.count)


class Parts:

    def __init__(self, nc, ctx):
        self.nc, self.ctx, self.stage = nc, ctx, ctx

    def sb(self, name, shape, dt=F32):
        return self.stage.enter_context(self.nc.sbuf_tensor(name, shape, dt))

    def sems(self, names):
        return {n: self.ctx.enter_context(self.nc.semaphore(n)) for n in names.split()}




def norm_parts(nc, k):
    k.norm_buf = k.sb("norm_buf", [P, 6 * CH])
    k.nsq, k.nstd, k.nrs = (k.norm_buf[:, 2 * i * CH:2 * (i + 1) * CH].rearrange("p (u t) -> p u t", u=2)
                            for i in range(3))
    k.N = k.sems("n_cen n_sq n_var n_std n_link n_out")


def norm_presets(nc, k):
    return {"tensor": [(k.N["n_var"], 2)], "scalar": [(k.N["n_std"], 2)], "vector": [(k.N["n_out"], 2)]}


def norm_pass(nc, k, index, src, dst, res=None, ready=None):
    N, bank = k.N, k.bank
    pairs = NCH // 2

    def pe_centre(pe, c, u):
        pe.wait_ge(N["n_out"], index * NCH + c + 1)
        nc.tensor.matmul(bank[u][:, :], k.centre[:, :], src[:, bass.ds(chunk_off(c), CH)],
                         start=True, stop=True).then_inc(N["n_cen"], 1)

    def pe_var(pe, c, u):
        pe.wait_ge(N["n_sq"], index * NCH + c + 1)
        pe.wait_ge(N["n_std"], index * NCH + c + 1)
        nc.tensor.matmul(bank[2 + u][:, :], k.mean[:, :], k.nsq[:, u, :],
                         start=True, stop=True).then_inc(N["n_var"], 1)

    def tensor(pe):
        if ready:
            pe.wait_ge(*ready)
        pe_centre(pe, 0, 0)
        with pe.Fori(0, pairs - 1) as p:
            for u in range(2):
                pe_centre(pe, p * 2 + u + 1, 1 - u)
                pe_var(pe, p * 2 + u, u)
        pe_centre(pe, NCH - 1, 1)
        pe_var(pe, NCH - 2, 0)
        pe_var(pe, NCH - 1, 1)

    def act_square(act, c, u):
        act.wait_ge(N["n_cen"], index * NCH + c + 1)
        act.wait_ge(N["n_var"], index * NCH + c + 1)
        nc.scalar.activation(k.nsq[:, u, :], bank[u][:, :], ACT.Square).then_inc(N["n_sq"], 1)

    def act_std(act, c, u):
        act.wait_ge(N["n_var"], index * NCH + c + 3)
        act.wait_ge(N["n_out"], index * NCH + c + 1)
        nc.scalar.activation(k.nstd[:, u, :], bank[2 + u][:, :], ACT.Sqrt,
                             bias=k.eps[:, 0:1]).then_inc(N["n_std"], 1)

    def scalar(act):
        act_square(act, 0, 0)
        with act.Fori(0, pairs - 1) as p:
            for u in range(2):
                act_square(act, p * 2 + u + 1, 1 - u)
                act_std(act, p * 2 + u, u)
        act_square(act, NCH - 1, 1)
        act_std(act, NCH - 2, 0)
        act_std(act, NCH - 1, 1)

    def vector(dve):
        links = 2 if res is not None else 1
        with dve.Fori(0, pairs) as p:
            for u in range(2):
                c = p * 2 + u
                dve.wait_ge(N["n_std"], index * NCH + c + 3)
                ch = Chain(dve, N["n_link"], k.norm_links + c * links)
                ch.link(nc.vector.reciprocal(k.nrs[:, u, :], k.nstd[:, u, :]))
                out = dst[:, bass.ds(chunk_off(c), CH)]
                if res is None:
                    nc.vector.tensor_tensor(out, bank[u][:, :], k.nrs[:, u, :], ALU.mult).then_inc(N["n_out"], 1)
                else:
                    ch.link(nc.vector.tensor_tensor(k.nrs[:, u, :], bank[u][:, :], k.nrs[:, u, :], ALU.mult))
                    nc.vector.tensor_tensor(out, k.nrs[:, u, :], res[:, bass.ds(chunk_off(c), CH)],
                                            ALU.add).then_inc(N["n_out"], 1)
        k.norm_links += NCH * links

    return {"tensor": tensor, "scalar": scalar, "vector": vector}


N_ST = 16
DT_RANK = 64
LOG1P_TERMS = 8


def ssm_stage(nc, k, dram):
    bank, x_a, x_b = k.bank, k.x_a, k.x_b
    sb = k.sb
    wx_dt = sb("wx_dt", [P, DT_RANK])
    wx_bc = sb("wx_bc", [P, 96])
    w_dt = sb("w_dt", [DT_RANK, D])
    avec = sb("avec", [P, N_ST + 2])
    a_neg = sb("a_neg", [P, N_ST])
    pick = sb("pick", [96, 2 * N_ST, P], BF16)
    dt = sb("dt", [P, T])
    dtu = sb("dtu", [P, T])
    bc3 = sb("bc3", [96, T], BF16)
    raw = sb("raw", [DT_RANK, CH])
    e_abs = sb("e_abs", [P, CH])
    relu = sb("relu", [P, CH])
    tmp = sb("tmp", [P, 3, CH])
    rest = sb("rest", [96, CH])
    a_bar = sb("a_bar", [P, 2, SLEN])
    b_rep = sb("b_rep", [P, 2, SLEN])
    dbu = sb("dbu", [P, 2, SLEN])
    h = sb("h", [P, 2, SLEN])
    hc = sb("hc", [P, 2, SLEN])
    S = k.sems("""a_loaded a_exp a_ready a_raw_mm a_raw a_dt_mm a_abs a_eabs a_relu a_bc_mm a_hi a_r1 a_mid a_r2 a_lo
        a_link a_q a_dt a_dtu a_b_mm a_b a_abar a_dbu a_c_mm a_scan a_hc a_y_mm a_out""")

    base = k.norm_index * NCH

    def sync(sp):
        for dst, src in ((wx_dt[:, :], "wx_dt"), (wx_bc[:, :], "wx_bc"), (w_dt[:, :], "w_dt"), (avec[:, :], "avec"),
                         (pick[:, :, :].bitcast(U16), "pick")):
            sp.dma_start(dst, dram[src]).then_inc(S["a_loaded"], 16)


    def tensor(pe):
        pe.wait_ge(S["a_loaded"], 80)
        pe.sem_inc(S["a_y_mm"], 2)
        pe.sem_inc(S["a_dt_mm"], 1)
        with pe.Fori(0, NCH) as c:
            pe.wait_ge(k.N["n_out"], base + c + 3)
            u = x_a[:, bass.ds(chunk_off(c), CH)]
            pe.wait_ge(S["a_raw"], c + 1)
            nc.tensor.matmul(bank[5][0:DT_RANK, :], wx_dt[:, :], u, start=True, stop=True).then_inc(S["a_raw_mm"], 1)
            pe.wait_ge(S["a_r1"], c + 1)
            nc.tensor.matmul(bank[4][0:96, :], wx_bc[:, :], u, start=True, stop=True).then_inc(S["a_bc_mm"], 1)
            pe.wait_ge(S["a_raw"], c + 2)
            pe.wait_ge(S["a_relu"], c + 1)
            nc.tensor.matmul(bank[6][:, :], w_dt[:, :], raw[:, :], start=True, stop=True).then_inc(S["a_dt_mm"], 1)
        pe.wait_ge(S["a_lo"], NCH)
        pe.wait_ge(S["a_relu"], NCH + 1)
        pe.wait_ge(S["a_r1"], NCH + 1)
        with pe.Fori(0, NSEQ) as s:
            def y_mm(n):
                for half in range(2):
                    pe.wait_ge(S["a_hc"], s * 32 + (2 * n + half + 3))
                    ins = nc.tensor.matmul(bank[2 + half][:, :], k.ident[:, :],
                                           hc[:, n % 2, half * CH:(half + 1) * CH], start=(n == 0),
                                           stop=(n == N_ST - 1))
                ins.then_inc(S["a_y_mm"], 1)

            for n in range(N_ST):
                for half in range(2):
                    rows = bc3[:, bass.ds(s * SLEN + half * CH, CH)]
                    pe.wait_ge(S["a_b"], s * 32 + (2 * n + half + 1))
                    nc.tensor.matmul(bank[4 + half][:, :], pick[:, n, :], rows, start=True,
                                     stop=True).then_inc(S["a_b_mm"], 1)
                for half in range(2):
                    rows = bc3[:, bass.ds(s * SLEN + half * CH, CH)]
                    pe.wait_ge(S["a_hc"], s * 32 + (2 * n + half + 1))
                    nc.tensor.matmul(bank[6 + half][:, :], pick[:, N_ST + n, :], rows, start=True,
                                     stop=True).then_inc(S["a_c_mm"], 1)
                if n == 1:
                    pe.wait_ge(S["a_out"], s * 2 + 1)
                if n >= 1:
                    y_mm(n - 1)
            y_mm(N_ST - 1)

    def scalar(act):
        act.sem_inc(S["a_raw"], 1)
        act.sem_inc(S["a_relu"], 1)
        act.sem_inc(S["a_b"], 2)
        act.wait_ge(S["a_loaded"], 80)
        nc.scalar.activation(a_neg[:, :], avec[:, 0:N_ST], ACT.Exp).then_inc(S["a_exp"], 1)
        with act.Fori(0, NCH) as c:
            act.wait_ge(S["a_raw_mm"], c + 1)
            act.wait_ge(S["a_dt_mm"], c + 1)
            nc.scalar.activation(raw[:, :], bank[5][0:DT_RANK, :], ACT.Copy).then_inc(S["a_raw"], 1)
            at = bass.ds(c * CH, CH)
            act.wait_ge(S["a_bc_mm"], c + 1)
            k.settle(act)
            nc.scalar.activation(bc3[:, at], bank[4][0:96, :], ACT.Copy).then_inc(S["a_hi"], 1)
            act.wait_ge(S["a_dt_mm"], c + 2)
            act.wait_ge(S["a_dt"], c + 1)
            nc.scalar.activation(e_abs[:, :], bank[6][:, :], ACT.Abs,
                                 bias=avec[:, N_ST:N_ST + 1]).then_inc(S["a_abs"], 1)
            nc.scalar.activation(relu[:, :], bank[6][:, :], ACT.Relu,
                                 bias=avec[:, N_ST:N_ST + 1]).then_inc(S["a_relu"], 1)
            act.wait_ge(S["a_abs"], c + 1)
            nc.scalar.activation(e_abs[:, :], e_abs[:, :], ACT.Exp, scale=-1.0).then_inc(S["a_eabs"], 1)
            act.wait_ge(S["a_r1"], c + 2)
            k.settle(act)
            nc.scalar.activation(bc3[32:64, at], rest[32:64, :], ACT.Copy)
            nc.scalar.activation(bc3[64:96, at], rest[64:96, :], ACT.Copy).then_inc(S["a_mid"], 1)
            act.wait_ge(S["a_r2"], c + 1)
            k.settle(act)
            nc.scalar.activation(bc3[64:96, at], rest[64:96, :], ACT.Copy).then_inc(S["a_lo"], 1)
        act.wait_ge(S["a_dt"], NCH + 1)
        act.wait_ge(S["a_ready"], 1)
        with act.Fori(0, NSEQ) as s:
            for n in range(N_ST):
                for half in range(2):
                    act.wait_ge(S["a_b_mm"], s * 32 + (2 * n + half + 1))
                    if half == 0:
                        act.wait_ge(S["a_dbu"], s * N_ST + (n + 1))
                    nc.scalar.activation(b_rep[:, n % 2, half * CH:(half + 1) * CH], bank[4 + half][:, :],
                                         ACT.Copy).then_inc(S["a_b"], 1)
                act.wait_ge(S["a_scan"], s * N_ST + (n + 1))
                k.settle(act)
                nc.scalar.activation(a_bar[:, n % 2, :], dt[:, bass.ds(s * SLEN, SLEN)], ACT.Exp,
                                     scale=a_neg[:, n:n + 1]).then_inc(S["a_abar"], 1)

    def vector(dve):
        dve.sem_inc(S["a_r1"], 1)
        dve.sem_inc(S["a_dt"], 1)
        dve.sem_inc(S["a_scan"], 2)
        dve.sem_inc(S["a_hc"], 2)
        dve.sem_inc(S["a_out"], 1)
        dve.wait_ge(S["a_exp"], 1)
        nc.vector.tensor_scalar(a_neg[:, :], a_neg[:, :], -1.0, None, ALU.mult).then_inc(S["a_ready"], 1)
        links = LOG1P_TERMS + 4
        with dve.Fori(0, NCH) as c:
            at = bass.ds(c * CH, CH)
            dve.wait_ge(S["a_hi"], c + 1)
            nc.vector.tensor_tensor(rest[:, :], bank[4][0:96, :], bc3[:, at], ALU.subtract).then_inc(S["a_r1"], 1)
            dve.wait_ge(S["a_mid"], c + 1)
            nc.vector.tensor_tensor(rest[64:96, :], rest[64:96, :], bc3[64:96, at],
                                    ALU.subtract).then_inc(S["a_r2"], 1)
            dve.wait_ge(S["a_eabs"], c + 1)
            ch = Chain(dve, S["a_link"], c * links)
            s1, s2, q = tmp[:, 0, :], tmp[:, 1, :], tmp[:, 2, :]
            ch.link(nc.vector.tensor_scalar(s1, e_abs[:, :], 2.0, None, ALU.add))
            ch.link(nc.vector.reciprocal(s2, s1))
            ch.link(nc.vector.tensor_tensor(s1, s2, e_abs[:, :], ALU.mult))
            ch.link(nc.vector.tensor_tensor(s2, s1, s1, ALU.mult))
            ch.link(nc.vector.tensor_scalar(q, s2, 1.0 / (2 * LOG1P_TERMS + 1), None, ALU.mult))
            for i in range(LOG1P_TERMS - 1, 0, -1):
                ch.link(nc.vector.scalar_tensor_tensor(out=q, in0=q, scalar=1.0 / (2 * i + 1), in1=s2, op0=ALU.add,
                                                       op1=ALU.mult))
            nc.vector.scalar_tensor_tensor(out=q, in0=q, scalar=1.0, in1=s1, op0=ALU.add,
                                           op1=ALU.mult).then_inc(S["a_q"], 1)
            dve.wait_ge(S["a_q"], c + 1)
            dve.wait_ge(S["a_relu"], c + 2)
            nc.vector.scalar_tensor_tensor(out=dt[:, at], in0=q, scalar=2.0, in1=relu[:, :], op0=ALU.mult,
                                           op1=ALU.add).then_inc(S["a_dt"], 1)
        with dve.Fori(0, NSEQ) as s:
            for n in range(N_ST):
                i = s * N_ST + n
                dve.wait_ge(S["a_abar"], i + 1)
                dve.wait_ge(S["a_dbu"], i + 3)
                nc.vector.tensor_tensor_scan(h[:, n % 2, :], a_bar[:, n % 2, :], dbu[:, n % 2, :], 0.0, ALU.mult,
                                             ALU.add).then_inc(S["a_scan"], 1)
                dve.wait_ge(S["a_scan"], i + 3)
                dve.wait_ge(S["a_y_mm"], i + 1)
                for half in range(2):
                    at = slice(half * CH, (half + 1) * CH)
                    dve.wait_ge(S["a_c_mm"], s * 32 + (2 * n + half + 1))
                    nc.vector.tensor_tensor(hc[:, n % 2, at], h[:, n % 2, at], bank[6 + half][:, :],
                                            ALU.mult).then_inc(S["a_hc"], 1)
            dve.wait_ge(S["a_y_mm"], s * N_ST + N_ST + 2)
            for half in range(2):
                at = bass.ds(s * SEQW + PAD + half * CH, CH)
                nc.vector.scalar_tensor_tensor(out=x_b[:, at], in0=x_a[:, at], scalar=avec[:, N_ST + 1:N_ST + 2],
                                               in1=bank[2 + half][:, :], op0=ALU.mult,
                                               op1=ALU.add).then_inc(S["a_out"], 1)

    def gpsimd(pool):
        pool.sem_inc(S["a_dbu"], 2)
        with pool.Fori(0, NCH) as c:
            pool.wait_ge(S["a_dt"], c + 2)
            k.settle(pool)
            nc.gpsimd.tensor_tensor(dtu[:, bass.ds(c * CH, CH)], dt[:, bass.ds(c * CH, CH)],
                                    x_a[:, bass.ds(chunk_off(c), CH)], ALU.mult).then_inc(S["a_dtu"], 1)
        pool.wait_ge(S["a_dtu"], NCH)
        with pool.Fori(0, NSEQ) as s:
            for n in range(N_ST):
                pool.wait_ge(S["a_b"], s * 32 + (2 * n + 4))
                pool.wait_ge(S["a_scan"], s * N_ST + (n + 1))
                k.settle(pool)
                nc.gpsimd.tensor_tensor(dbu[:, n % 2, :], dtu[:, bass.ds(s * SLEN, SLEN)], b_rep[:, n % 2, :],
                                        ALU.mult).then_inc(S["a_dbu"], 1)

    k.stage_done = (S["a_out"], 2 * NSEQ + 1)
    return {"sync": sync, "tensor": tensor, "scalar": scalar, "vector": vector, "gpsimd": gpsimd}


EXPERTS = 8
FU = 512
UT = FU // P
TB = T // P


def moe_stage(nc, k, dram):
    bank, x_a, x_b, ident = k.bank, k.x_a, k.x_b, k.ident
    sb = k.sb
    w_r = sb("w_router", [P, EXPERTS])
    w_up = sb("w_up", [P, EXPERTS, FU])
    w_dn = sb("w_dn", [P, EXPERTS, UT, D])
    evec = sb("evec", [P, EXPERTS, UT + 1])
    rank = sb("rank", [P, TB, EXPERTS])
    pick8 = sb("pick8", [3 * EXPERTS, EXPERTS, P], BF16)
    logit_t = sb("logit_t", [EXPERTS, 2, CH])
    logits = sb("logits", [P, TB, EXPERTS])
    work = sb("work", [P, 4, TB, EXPERTS])
    top = sb("top", [P, 4, TB])
    gate_w = sb("gate_w", [P, TB, EXPERTS])
    gate3 = sb("gate3", [P, TB, 3, EXPERTS], BF16)
    gate_t = sb("gate_t", [3 * EXPERTS, T], BF16)
    ident_bf = sb("moe_ident_bf", [P, P], BF16)
    hid = sb("moe_hid", [P, 2, UT, CH])
    gate_b = sb("gate_b", [P, 2, CH])
    part = sb("part", [P, 2, CH])
    acc = sb("acc", [P, 2, CH])
    S = k.sems("""b_loaded b_logit_mm b_logit_t b_logit_tr b_logits b_link b_exp b_gate_w b_rest b_gates b_gate_tr b_gate_t
        b_up_mm b_hid b_dn_mm b_gate_mm b_gate b_part b_acc""")
    base = k.norm_index * NCH
    trf = k.bank_bf

    def sync(sp):
        for dst, src in ((w_r[:, :], "w_router"), (w_up[:, :, :], "w_up"), (w_dn[:, :, :, :], "w_dn"),
                         (evec[:, :, :], "evec"), (rank[:, :, :], "rank"), (pick8[:, :, :].bitcast(U16), "pick8"),
                         (ident_bf[:, :].bitcast(U16), "ident_bf")):
            sp.dma_start(dst, dram[src]).then_inc(S["b_loaded"], 16)

    def tensor(pe):
        pe.sem_inc(S["b_logit_mm"], 1)
        pe.sem_inc(S["b_logit_tr"], 1)
        pe.sem_inc(S["b_dn_mm"], 2)
        pe.wait_ge(S["b_loaded"], 112)
        with pe.Fori(0, NCH) as c:
            pe.wait_ge(k.N["n_out"], base + c + 3)
            pe.wait_ge(S["b_logit_t"], c + 1)
            nc.tensor.matmul(bank[4][0:EXPERTS, :], w_r[:, :], x_a[:, bass.ds(chunk_off(c), CH)], start=True,
                             stop=True).then_inc(S["b_logit_mm"], 1)
            pe.wait_ge(S["b_logit_t"], c + 2)
            pe.wait_ge(S["b_logits"], c + 1)
            k.settle(pe)
            for j in range(CH // P):
                ins = nc.tensor.transpose(bank[5][:, j * EXPERTS:(j + 1) * EXPERTS],
                                          logit_t[:, 0, j * P:(j + 1) * P], ident[0:EXPERTS, 0:EXPERTS])
            ins.then_inc(S["b_logit_tr"], 1)
        pe.wait_ge(S["b_gates"], 3)
        for b in range(TB):
            ins = nc.tensor.transpose(trf[4 + b // 8][0:3 * EXPERTS, (b % 8) * P:(b % 8 + 1) * P],
                                      gate3[:, b, :, :].rearrange("p a e -> p (a e)"), ident_bf[:, :])
            if b % 8 == 7:
                ins.then_inc(S["b_gate_tr"], 1)
        pe.wait_ge(S["b_gate_t"], 4)

        def down(c, e):
            i = c * EXPERTS + e
            pe.wait_ge(S["b_part"], i + 1)
            for j in range(UT):
                pe.wait_ge(S["b_hid"], i * UT + (j + 5))
                ins = nc.tensor.matmul(bank[4 + e % 2][:, :], w_dn[:, e, j, :], hid[:, e % 2, j, :], start=(j == 0),
                                       stop=(j == UT - 1))
            ins.then_inc(S["b_dn_mm"], 1)

        with pe.Fori(0, NCH) as c:
            for e in range(EXPERTS):
                i = c * EXPERTS + e
                for j in range(UT):
                    pe.wait_ge(S["b_hid"], i * UT + (j + 1))
                    nc.tensor.matmul(bank[j][:, :], w_up[:, e, j * P:(j + 1) * P],
                                     x_a[:, bass.ds(chunk_off(c), CH)], start=True,
                                     stop=True).then_inc(S["b_up_mm"], 1)
                pe.wait_ge(S["b_gate"], i + 1)
                k.settle(pe)
                nc.tensor.matmul(bank[6 + e % 2][:, :], pick8[:, e, :], gate_t[:, bass.ds(c * CH, CH)], start=True,
                                 stop=True).then_inc(S["b_gate_mm"], 1)
                if e >= 1:
                    down(c, e - 1)
            down(c, EXPERTS - 1)

    def scalar(act):
        act.sem_inc(S["b_logit_t"], 1)
        act.sem_inc(S["b_logits"], 1)
        act.sem_inc(S["b_hid"], 4)
        act.sem_inc(S["b_gate"], 2)
        act.wait_ge(S["b_loaded"], 112)
        with act.Fori(0, NCH) as c:
            act.wait_ge(S["b_logit_mm"], c + 2)
            act.wait_ge(S["b_logit_tr"], c + 1)
            nc.scalar.activation(logit_t[:, 0, :], bank[4][0:EXPERTS, :], ACT.Copy).then_inc(S["b_logit_t"], 1)
            act.wait_ge(S["b_logit_tr"], c + 2)
            k.settle(act)
            nc.scalar.activation(logits[:, bass.ds(c * (CH // P), CH // P), :],
                                 bank[5][:, 0:CH // P * EXPERTS].rearrange("p (b e) -> p b e", e=EXPERTS),
                                 ACT.Copy).then_inc(S["b_logits"], 1)
        act.wait_ge(S["b_link"], 9)
        nc.scalar.activation(top[:, 2, :], top[:, 2, :], ACT.Exp).then_inc(S["b_exp"], 1)
        act.wait_ge(S["b_gate_w"], 1)
        nc.scalar.activation(gate3[:, :, 0, :], gate_w[:, :, :], ACT.Copy).then_inc(S["b_gates"], 1)
        act.wait_ge(S["b_rest"], 1)
        nc.scalar.activation(gate3[:, :, 1, :], work[:, 0, :, :], ACT.Copy).then_inc(S["b_gates"], 1)
        act.wait_ge(S["b_rest"], 2)
        nc.scalar.activation(gate3[:, :, 2, :], work[:, 1, :, :], ACT.Copy).then_inc(S["b_gates"], 1)
        for q in range(4):
            act.wait_ge(S["b_gate_tr"], q + 1)
            nc.scalar.activation(gate_t[:, q * 8 * P:(q + 1) * 8 * P], trf[4 + q][0:3 * EXPERTS, 0:8 * P],
                                 ACT.Copy).then_inc(S["b_gate_t"], 1)
        with act.Fori(0, NCH) as c:
            for e in range(EXPERTS):
                i = c * EXPERTS + e
                act.wait_ge(S["b_dn_mm"], i + 1)
                for j in range(UT):
                    act.wait_ge(S["b_up_mm"], i * UT + (j + 1))
                    nc.scalar.activation(hid[:, e % 2, j, :], bank[j][:, :], ACT.Gelu,
                                         bias=evec[:, e, j:j + 1]).then_inc(S["b_hid"], 1)
                act.wait_ge(S["b_gate_mm"], i + 1)
                act.wait_ge(S["b_part"], i + 1)
                nc.scalar.activation(gate_b[:, e % 2, :], bank[6 + e % 2][:, :], ACT.Copy).then_inc(S["b_gate"], 1)

    def vector(dve):
        dve.sem_inc(S["b_part"], 2)
        dve.wait_ge(S["b_logits"], NCH + 1)
        dve.wait_ge(S["b_loaded"], 112)
        ch = Chain(dve, S["b_link"], 0)

        def one_of(src, hot, best):
            ch.link(nc.vector.tensor_reduce(best, src, AX, ALU.max))
            ch.link(nc.vector.tensor_tensor(hot, src, best.unsqueeze(2).broadcast_to([P, TB, EXPERTS]), ALU.is_equal))
            ch.link(nc.vector.tensor_tensor(hot, hot, rank[:, :, :], ALU.mult))
            ch.link(nc.vector.tensor_reduce(top[:, 3, :], hot, AX, ALU.max))

        wide = lambda a: a.unsqueeze(2).broadcast_to([P, TB, EXPERTS])
        hot1, hot2, rest = work[:, 0, :, :], work[:, 1, :, :], work[:, 2, :, :]
        one_of(logits[:, :, :], hot1, top[:, 0, :])
        ch.link(nc.vector.tensor_tensor(hot1, rank[:, :, :], wide(top[:, 3, :]), ALU.is_equal))
        ch.link(nc.vector.scalar_tensor_tensor(out=rest, in0=hot1, scalar=-3e38, in1=logits[:, :, :], op0=ALU.mult,
                                               op1=ALU.add))
        ch.link(nc.vector.tensor_reduce(top[:, 1, :], rest, AX, ALU.max))
        ch.link(nc.vector.tensor_tensor(hot2, rest, wide(top[:, 1, :]), ALU.is_equal))
        ch.link(nc.vector.tensor_tensor(top[:, 2, :], top[:, 1, :], top[:, 0, :], ALU.subtract))
        ch.link(nc.vector.tensor_tensor(hot2, hot2, rank[:, :, :], ALU.mult))
        ch.link(nc.vector.tensor_reduce(top[:, 3, :], hot2, AX, ALU.max))
        ch.link(nc.vector.tensor_tensor(hot2, rank[:, :, :], wide(top[:, 3, :]), ALU.is_equal))
        dve.wait_ge(S["b_exp"], 1)
        ch.link(nc.vector.tensor_scalar(top[:, 0, :], top[:, 2, :], 1.0, None, ALU.add))
        ch.link(nc.vector.reciprocal(top[:, 1, :], top[:, 0, :]))
        ch.link(nc.vector.tensor_tensor(top[:, 2, :], top[:, 2, :], top[:, 1, :], ALU.mult))
        ch.link(nc.vector.tensor_tensor(hot1, hot1, wide(top[:, 1, :]), ALU.mult))
        ch.link(nc.vector.tensor_tensor(hot2, hot2, wide(top[:, 2, :]), ALU.mult))
        nc.vector.tensor_tensor(gate_w[:, :, :], hot1, hot2, ALU.add).then_inc(S["b_gate_w"], 1)
        dve.wait_ge(S["b_gates"], 1)
        nc.vector.tensor_tensor(work[:, 0, :, :], gate_w[:, :, :], gate3[:, :, 0, :], ALU.subtract).then_inc(S["b_rest"], 1)
        dve.wait_ge(S["b_rest"], 1)
        dve.wait_ge(S["b_gates"], 2)
        nc.vector.tensor_tensor(work[:, 1, :, :], work[:, 0, :, :], gate3[:, :, 1, :],
                                ALU.subtract).then_inc(S["b_rest"], 1)
        with dve.Fori(0, NCH) as c:
            for e in range(EXPERTS):
                i = c * EXPERTS + e
                dve.wait_ge(S["b_dn_mm"], i + 3)
                dve.wait_ge(S["b_gate"], i + 3)
                dve.wait_ge(S["b_acc"], i + 1)
                nc.vector.scalar_tensor_tensor(out=part[:, e % 2, :], in0=bank[4 + e % 2][:, :],
                                               scalar=evec[:, e, UT:UT + 1], in1=gate_b[:, e % 2, :], op0=ALU.add,
                                               op1=ALU.mult).then_inc(S["b_part"], 1)

    def gpsimd(pool):
        pool.sem_inc(S["b_acc"], 2)
        with pool.Fori(0, NCH) as c:
            for e in range(EXPERTS):
                i = c * EXPERTS + e
                if e == 0:
                    continue
                pool.wait_ge(S["b_part"], i + 3)
                if e > 1:
                    pool.wait_ge(S["b_acc"], i + 2)
                first = part[:, 0, :] if e == 1 else acc[:, (e - 1) % 2, :]
                out = x_b[:, bass.ds(chunk_off(c), CH)] if e == EXPERTS - 1 else acc[:, e % 2, :]
                if e == EXPERTS - 1:
                    k.settle(pool)
                ins = nc.gpsimd.tensor_tensor(out, first, part[:, e % 2, :], ALU.add)
                ins.then_inc(S["b_acc"], 2 if e == 1 else 1)

    k.stage_done = (S["b_acc"], EXPERTS * NCH + 2)
    return {"sync": sync, "tensor": tensor, "scalar": scalar, "vector": vector, "gpsimd": gpsimd}


TAPS = 31
WCOLS = 512
WG = WCOLS // 32
PE_ADDS = (TAPS + 1) // 2
POOL_ADDS = TAPS // 2
CB = CH // P


def conv_stage(nc, k, dram):
    bank, x_a, x_b = k.bank, k.x_a, k.x_b
    sb = k.sb
    w_lin = sb("w_lin", [P, TAPS * HEADS])
    spread = sb("spread", [96, 2, P], BF16)
    ident_bf = sb("conv_ident_bf", [P, P], BF16)
    xc = sb("xc", [P, 2, CH])
    w = sb("conv_w", [P, CB, WCOLS])
    w_rest = sb("conv_rest", [P, CB, WCOLS])
    w3 = sb("conv_w3", [P, CB, WG, 3, 32], BF16)
    w_t = sb("conv_wt", [96, 2, WG, CH], BF16)
    mx = sb("conv_max", [P, CB, HEADS])
    sm = sb("conv_sum", [P, CB, HEADS])
    inv = sb("conv_inv", [P, CB, HEADS])
    pe_prod = sb("pe_prod", [P, 2, CH])
    pool_prod = sb("pool_prod", [P, 2, CH])
    acc = sb("conv_acc", [P, CH])
    S = k.sems("""v_loaded v_zero v_xc v_log_mm v_link v_sub v_exp v_norm v_hi v_r1 v_mid v_r2 v_lo v_tr v_wt
        v_tap_mm v_prod v_add_mm v_add v_out""")
    base = k.norm_index * NCH
    by_head = lambda a: a.rearrange("p (k h) -> p h k", h=HEADS)
    by_group = lambda a: a.rearrange("p (g i) -> p g i", g=WG)
    LIVE = TAPS * HEADS

    def sync(sp):
        for dst, src in ((w_lin[:, :], "w_lin"), (spread[:, :, :].bitcast(U16), "spread"), (ident_bf[:, :].bitcast(U16), "ident_bf")):
            sp.dma_start(dst, dram[src]).then_inc(S["v_loaded"], 16)


    def pool_copy(pool, c, u):
        pool.wait_ge(k.N["n_out"], base + c + 3)
        pool.wait_ge(S["v_log_mm"], c * CB + 4)
        k.settle(pool)
        nc.gpsimd.tensor_copy(xc[:, u, :], x_a[:, bass.ds(chunk_off(c), CH)]).then_inc(S["v_xc"], 1)

    def pe_logits(pe, c, u):
        pe.wait_ge(S["v_xc"], c + 1)
        for b in range(CB):
            pe.wait_ge(S["v_sub"], c * CB + (b + 1))
            nc.tensor.matmul(bank[b % 2][:, 0:LIVE], xc[:, u, b * P:(b + 1) * P], w_lin[:, :], start=True,
                             stop=True).then_inc(S["v_log_mm"], 1)

    def dve_weights(dve, c, u):
        ch = Chain(dve, S["v_link"], c * (3 * CB))
        for b in range(CB):
            dve.wait_ge(S["v_log_mm"], c * CB + (b + 9))
            lo = bank[b % 2][:, 0:LIVE]
            ch.link(nc.vector.tensor_reduce(mx[:, b, :], by_head(lo), AX, ALU.max))
            dve.wait_ge(S["v_r1"], c * CB + (b + 1))
            nc.vector.tensor_tensor(by_head(w[:, b, 0:LIVE]), by_head(lo),
                                    mx[:, b, :].unsqueeze(2).broadcast_to([P, HEADS, TAPS]),
                                    ALU.subtract).then_inc(S["v_sub"], 1)
        for b in range(CB):
            dve.wait_ge(S["v_exp"], c * CB + (b + 1))
            live = by_head(w[:, b, 0:LIVE])
            ch.link(nc.vector.tensor_reduce(sm[:, b, :], live, AX, ALU.add))
            ch.link(nc.vector.reciprocal(inv[:, b, :], sm[:, b, :]))
            nc.vector.tensor_tensor(live, live, inv[:, b, :].unsqueeze(2).broadcast_to([P, HEADS, TAPS]),
                                    ALU.mult).then_inc(S["v_norm"], 1)

    def act_weights(act, c, u):
        for b in range(CB):
            act.wait_ge(S["v_sub"], c * CB + (b + 3))
            nc.scalar.activation(w[:, b, 0:LIVE], w[:, b, 0:LIVE], ACT.Exp).then_inc(S["v_exp"], 1)
        for part, ready, lag, done in ((0, "v_norm", 1, "v_hi"), (1, "v_r1", 5, "v_mid"), (2, "v_r2", 1, "v_lo")):
            for b in range(CB):
                act.wait_ge(S[ready], c * CB + (b + lag))
                if part == 0:
                    act.wait_ge(S["v_tr"], c * 2 * CB + (2 * b + 2))
                src = (w if part == 0 else w_rest)[:, b, :]
                nc.scalar.activation(w3[:, b, :, part, :], by_group(src), ACT.Copy).then_inc(S[done], 1)

    def pool_rest(pool, c, u, i):
        b = i % CB
        if i < CB:
            pool.wait_ge(S["v_hi"], c * CB + (b + 1))
            pool.wait_ge(S["v_lo"], c * CB + (b + 1))
            nc.gpsimd.tensor_tensor(by_group(w_rest[:, b, :]), by_group(w[:, b, :]), w3[:, b, :, 0, :],
                                    ALU.subtract).then_inc(S["v_r1"], 1)
        else:
            pool.wait_ge(S["v_mid"], c * CB + (b + 1))
            nc.gpsimd.tensor_tensor(by_group(w_rest[:, b, :]), by_group(w_rest[:, b, :]), w3[:, b, :, 1, :],
                                    ALU.subtract).then_inc(S["v_r2"], 1)

    def pe_turn(pe, c, u, j):
        b, half = j // 2, j % 2
        pe.wait_ge(S["v_lo"], c * CB + (b + 5))
        pe.wait_ge(S["v_wt"], c * 2 * CB + (j + 1))
        for g in range(WG // 2):
            ins = nc.tensor.transpose(k.bank_bf[2 + half][0:96, g * P:(g + 1) * P],
                                      w3[:, b, half * (WG // 2) + g, :, :].rearrange("p a i -> p (a i)"),
                                      ident_bf[:, :])
        ins.then_inc(S["v_tr"], 1)

    def act_turn(act, c, u):
        act.wait_ge(S["v_tap_mm"], c * TAPS + TAPS)
        for j in range(2 * CB):
            b, half = j // 2, j % 2
            act.wait_ge(S["v_tr"], c * 2 * CB + (j + 9))
            nc.scalar.activation(w_t[:, u, half * (WG // 2):(half + 1) * (WG // 2), b * P:(b + 1) * P],
                                 k.bank_bf[2 + half][0:96, :].rearrange("p (g t) -> p g t", t=P),
                                 ACT.Copy).then_inc(S["v_wt"], 1)


    def pe_add(pe, c, u, tap):
        pe.wait_ge(S["v_prod"], c * TAPS + (tap + 3))
        if tap == 0:
            pe.wait_ge(S["v_out"], c + 1)
        nc.tensor.matmul(bank[7][:, :], k.ident[:, :], pe_prod[:, (tap // 2) % 2, :], start=(tap == 0),
                         stop=(tap == TAPS - 1)).then_inc(S["v_add_mm"], 1)

    def pe_taps(pe, c, u, more):
        pe.wait_ge(S["v_wt"], c * 2 * CB + (2 * CB + 2))
        for tap in range(TAPS):
            pe.wait_ge(S["v_prod"], c * TAPS + (tap + 1))
            nc.tensor.matmul(bank[4 + (u + tap) % 2][:, :], spread[:, tap % 2, :], w_t[:, u, tap // 2, :], start=True,
                             stop=True).then_inc(S["v_tap_mm"], 1)
            if tap >= 2 and tap % 2 == 0:
                pe_add(pe, c, u, tap - 2)
            if more and tap >= 14 and tap % 2 == 0 and tap < 14 + 4 * CB:
                pe_turn(pe, c + 1, 1 - u, (tap - 14) // 2)
        pe_add(pe, c, u, TAPS - 1)

    def dve_taps(dve, c, u):
        for tap in range(TAPS):
            dve.wait_ge(S["v_tap_mm"], c * TAPS + (tap + 1 + 2 * TAPS))
            if tap % 2 == 0:
                dve.wait_ge(S["v_add_mm"], c * PE_ADDS + (tap // 2 + 1))
                out = pe_prod[:, (tap // 2) % 2, :]
            else:
                dve.wait_ge(S["v_add"], c * POOL_ADDS + (tap // 2 + 1))
                out = pool_prod[:, (u + tap // 2) % 2, :]
            x = x_a[:, bass.ds(chunk_off(c) + tap - (TAPS - 1), CH)]
            nc.vector.tensor_tensor(out, x, bank[4 + (u + tap) % 2][:, :], ALU.mult).then_inc(S["v_prod"], 1)
        dve.wait_ge(S["v_add_mm"], c * PE_ADDS + (PE_ADDS + 2))
        dve.wait_ge(S["v_add"], c * POOL_ADDS + (POOL_ADDS + 2))
        nc.vector.tensor_tensor(x_b[:, bass.ds(chunk_off(c), CH)], acc[:, :], bank[7][:, :],
                                ALU.add).then_inc(S["v_out"], 1)

    def pool_taps(pool, c, u, more):
        for i in range(POOL_ADDS):
            if i > 0:
                pool.wait_ge(S["v_prod"], c * TAPS + (2 * i + 4))
                if i == 1:
                    pool.wait_ge(S["v_out"], c + 1)
                else:
                    pool.wait_ge(S["v_add"], c * POOL_ADDS + (i + 2))
                first = pool_prod[:, u, :] if i == 1 else acc[:, :]
                nc.gpsimd.tensor_tensor(acc[:, :], first, pool_prod[:, (u + i) % 2, :],
                                        ALU.add).then_inc(S["v_add"], 2 if i == 1 else 1)
            if more and i < 2 * CB:
                pool_rest(pool, c + 1, 1 - u, i)

    def steps(eng, weights, taps):
        weights(eng, 0, 0)
        with eng.Fori(0, NCH // 2 - 1) as pair:
            for u in range(2):
                weights(eng, pair * 2 + (u + 1), 1 - u)
                taps(eng, pair * 2 + u, u, True)
        weights(eng, NCH - 1, 1)
        taps(eng, NCH - 2, 0, True)
        taps(eng, NCH - 1, 1, False)

    def tensor(pe):
        pe.sem_inc(S["v_log_mm"], 8)
        pe.sem_inc(S["v_tr"], 8)
        pe.sem_inc(S["v_tap_mm"], 2 * TAPS)
        pe.sem_inc(S["v_add_mm"], 2)
        pe.wait_ge(S["v_loaded"], 48)
        pe.wait_ge(k.N["n_out"], base + NCH + 2)
        pe_logits(pe, 0, 0)
        for j in range(2 * CB):
            pe_turn(pe, 0, 0, j)
        with pe.Fori(0, NCH // 2 - 1) as pair:
            for u in range(2):
                pe_logits(pe, pair * 2 + (u + 1), 1 - u)
                pe_taps(pe, pair * 2 + u, u, True)
        pe_logits(pe, NCH - 1, 1)
        pe_taps(pe, NCH - 2, 0, True)
        pe_taps(pe, NCH - 1, 1, False)

    def scalar(act):
        act.sem_inc(S["v_lo"], 4)
        act.sem_inc(S["v_wt"], 2)
        act.wait_ge(S["v_zero"], 1)

        def weights(act, c, u):
            act_weights(act, c, u)
            act_turn(act, c, u)

        steps(act, weights, lambda *a: None)

    def vector(dve):
        dve.sem_inc(S["v_sub"], 2)
        dve.sem_inc(S["v_prod"], 2)
        dve.sem_inc(S["v_out"], 1)
        steps(dve, dve_weights, lambda dve, c, u, more: dve_taps(dve, c, u))

    def gpsimd(pool):
        pool.sem_inc(S["v_r1"], 4)
        pool.sem_inc(S["v_add"], 2)
        nc.gpsimd.memset(w[:, :, LIVE:], 0.0).then_inc(S["v_zero"], 1)
        pool.wait_ge(S["v_zero"], 1)
        pool_copy(pool, 0, 0)
        pool_copy(pool, 1, 1)
        for i in range(2 * CB):
            pool_rest(pool, 0, 0, i)
        with pool.Fori(0, NCH // 2 - 1) as pair:
            for u in range(2):
                pool_taps(pool, pair * 2 + u, u, True)
                pool_copy(pool, pair * 2 + (u + 2), u)
        pool_taps(pool, NCH - 2, 0, True)
        pool_taps(pool, NCH - 1, 1, False)

    k.stage_done = (S["v_out"], NCH + 1)
    return {"sync": sync, "tensor": tensor, "scalar": scalar, "vector": vector, "gpsimd": gpsimd}



def layers_stage(nc, k, dram, norm_index):
    bank, x_a, x_b, ident = k.bank, k.x_a, k.x_b, k.ident
    sb = k.sb
    w_qk = sb("w_qk", [P, 2 * INNER])
    wv_t = sb("wv_t", [P, HP, D])
    w_o = sb("w_o", [P, HP, D])
    w_vo = sb("w_vo", [P, HEADS, D])
    rot = sb("rot", [P, BPS, 256])
    rot_scale = sb("rot_scale", [P, 256])
    xs = sb("xs", [P, 2, WIN + BLK])
    xs2 = sb("xs2", [P, 2, 4, 2, 2 * WIN])
    qk_raw = sb("qk_raw", [P, 2, 2 * INNER])
    qk_sq = sb("qk_sq", [P, 2 * INNER])
    rot_b = sb("rot_b", [P, 2 * INNER])
    qk_rot = sb("qk_rot", [P, 2, 2 * INNER])
    norm2 = sb("norm2", [P, 2, 32])
    rnorm = sb("rnorm", [P, 2, 32])
    minus_half = sb("minus_half", [P, 32])
    q_z = sb("q_z", [P, 2, HP, 4, 2, WIN])
    k_t = sb("k_t", [P, 2, HP, WIN + BLK])
    x_keys = sb("x_keys", [P, 2, 4, D])
    prob = sb("prob", [P, 2, 2, CH])
    row_max = sb("row_max", [P, 16])
    row_sum = sb("row_sum", [P, 16])
    row_inv = sb("row_inv", [P, 2, 16])
    prob_t = sb("prob_t", [P, 2, 4, P])
    y_t = k.norm_buf[:, 0:HEADS * BLK].rearrange("p (h t) -> p h t", h=HEADS)
    xf, xn, gate = (qk_rot[:, :, :].rearrange("p a (b t) -> p (a b t)", t=CH)[:, 2 * i * CH:2 * (i + 1) * CH]
                    .rearrange("p (u t) -> p u t", u=2) for i in range(3))
    hid = qk_sq[:, 0:3 * CH].rearrange("p (j t) -> p j t", j=3)
    o_t = sb("o_t", [P, 2, BLK])
    ident_bf = sb("ident_bf", [P, P], BF16)
    w1 = sb("w1", [P, 2 * FI])
    w2 = sb("w2", [P, 3, D])
    fvec = sb("fvec", [P, 9])

    S = k.sems("""const_loaded qk_loaded vo_loaded scale_loaded ffn_loaded layer_init
        vo_done vo_evac rot_ready shift_link xs_ready
        proj_done proj_evac sq_done sq_summed rn_ready rotb_ready rot_link rotb_used rope_ready
        tr_done tr_evac tail_ready sim_done sub_ready sm_link exp_ready inv_ready prob_ready
        c_done c_evac pool_link xb_ready
        f_shift_link f_xs f_cen f_sq f_var f_std f_link f_xn f_gate_mm f_a_mm f_gate f_hid f_out_mm xa_ready""")


    def pool_shift(pool, g, n, u):
        pool.wait_ge(S["tr_done"], g * 5 + 1)
        if not isinstance(n, int) or n >= 3:
            pool.wait_ge(S["prob_ready"], g)
        elif n > 0:
            pool.wait_ge(S["rn_ready"], g)
        ch = Chain(pool, S["shift_link"], g * 2)
        k.settle(pool)
        ch.link(nc.gpsimd.tensor_copy(xs[0:64, u, :], x_a[0:64, bass.ds(blk_off(n) - WIN, WIN + BLK)]))
        k.settle(pool)
        ch.link(nc.gpsimd.tensor_copy(xs[64:128, u, :], x_a[64:128, bass.ds(blk_off(n) - WIN - 1, WIN + BLK)]))
        k.settle(pool)
        for dup in range(2):
            ins = nc.gpsimd.tensor_copy(xs2[:, u, :, dup, 0:WIN],
                                        xs[:, u, 0:BLK].rearrange("p (w c) -> p w c", w=4))
            ins = nc.gpsimd.tensor_copy(xs2[:, u, :, dup, WIN:2 * WIN],
                                        xs[:, u, WIN:WIN + BLK].rearrange("p (w c) -> p w c", w=4))
        ins.then_inc(S["xs_ready"], 1)

    def pe_project(pe, g, n, u):
        pe.wait_ge(S["xs_ready"], g + 1)
        for j in range(4):
            pe.wait_ge(S["proj_evac"], g * 4 + j + 1)
            nc.tensor.matmul(bank[j % 2][:, :], xs[:, u, WIN:WIN + BLK], w_qk[:, j * CH:(j + 1) * CH],
                             start=True, stop=True).then_inc(S["proj_done"], 1)

    def act_project(act, g, n, u):
        act.wait_ge(S["rope_ready"], g + 1)
        for j in range(4):
            act.wait_ge(S["proj_done"], g * 4 + j + 1)
            nc.scalar.activation(qk_raw[:, u, j * CH:(j + 1) * CH], bank[j % 2][:, :],
                                 ACT.Copy).then_inc(S["proj_evac"], 1)
        act.wait_ge(S["sq_summed"], g + 1)
        act.wait_ge(S["proj_evac"], g * 4 + 6)
        nc.scalar.activation(qk_sq[:, :], qk_raw[:, u, :], ACT.Square).then_inc(S["sq_done"], 1)

    def dve_rope(dve, g, n, u):
        dve.wait_ge(S["sq_done"], g + 1)
        nc.vector.tensor_reduce(norm2[:, u, :], qk_sq[:, :].rearrange("p (h d) -> p h d", d=DH), AX,
                                ALU.add).then_inc(S["sq_summed"], 1)
        dve.wait_ge(S["tr_done"], g * 5 + 5)
        dve.wait_ge(S["proj_evac"], g * 4 + 6)
        ch = Chain(dve, S["rot_link"], g * 2 + 2)
        cos = rot[:, bass.ds(n % BPS, 1), 0:128].rearrange("p o (q d) -> p (o q) d", q=2)
        out = qk_rot[:, u, :].rearrange("p (q h d) -> p q h d", q=2, d=DH)
        ch.link(nc.vector.tensor_tensor(out, qk_raw[:, u, :].rearrange("p (q h d) -> p q h d", q=2, d=DH),
                                        cos.unsqueeze(2).broadcast_to([P, 2, HEADS, DH]), ALU.mult))
        dve.wait_ge(S["rotb_ready"], g + 1)
        ch.link(nc.vector.tensor_tensor(qk_rot[:, u, :], qk_rot[:, u, :], rot_b[:, :], ALU.add))
        dve.wait_ge(S["rn_ready"], g + 1)
        flat = qk_rot[:, u, :].rearrange("p (h d) -> p h d", d=DH)
        nc.vector.tensor_tensor(flat, flat, rnorm[:, u, :].unsqueeze(2).broadcast_to([P, 32, DH]),
                                ALU.mult).then_inc(S["rope_ready"], 1)

    def pool_rope(pool, g, n, u):
        pool.wait_ge(S["proj_evac"], g * 4 + 6)
        pool.wait_ge(S["rot_link"], g * 2 + 2)
        src = qk_raw[:, u, :].rearrange("p (q h d) -> p q h d", q=2, d=DH)
        dst = rot_b[:, :].rearrange("p (q h d) -> p q h d", q=2, d=DH)
        sin = rot[:, bass.ds(n % BPS, 1), 128:256].rearrange("p o (q d) -> p (o q) d", q=2)
        for d0, s0 in ((0, DH // 2), (DH // 2, 0)):
            for q in range(2):
                ins = nc.gpsimd.tensor_tensor(
                    dst[:, q, :, d0:d0 + DH // 2], src[:, q, :, s0:s0 + DH // 2],
                    sin[:, q:q + 1, d0:d0 + DH // 2].broadcast_to([P, HEADS, DH // 2]), ALU.mult)
        ins.then_inc(S["rotb_ready"], 1)
        pool.wait_ge(S["sq_summed"], g + 2)
        pool.wait_ge(S["rope_ready"], g + 1)
        ch = Chain(pool, S["pool_link"], g)
        k.settle(pool)
        ch.link(nc.gpsimd.tensor_scalar(norm2[:, u, :], norm2[:, u, :], 1e-24, None, ALU.max))
        nc.gpsimd.tensor_tensor(rnorm[:, u, :], norm2[:, u, :], minus_half[:, :],
                                ALU.pow).then_inc(S["rn_ready"], 1)

    def pe_scores(pe, g, n, u):
        pe.wait_ge(S["tr_evac"], g * 5 + 1)
        for w in range(4):
            ins = nc.tensor.transpose(bank[2 + u][:, w * D:(w + 1) * D],
                                      xs2[:, u, w, :, :].rearrange("p a b -> p (a b)"), ident[:, :])
        ins.then_inc(S["tr_done"], 1)
        pe.wait_ge(S["rope_ready"], g + 3)
        for j in range(4):
            pe.wait_ge(S["tr_evac"], g * 5 + 2 + j)
            for m in range(4):
                ins = nc.tensor.transpose(bank[2 + (u + 1 + j) % 2][:, m * P:(m + 1) * P],
                                          qk_rot[:, u, (4 * j + m) * P:(4 * j + m + 1) * P], ident[:, :])
            ins.then_inc(S["tr_done"], 1)
        pe.wait_ge(S["sub_ready"], g + 1)
        pe.wait_ge(S["tr_evac"], g * 5 + 7)
        pe.wait_ge(S["tail_ready"], g + 1)
        for wb in range(2):
            m_rhs = k.mask_by_block[:, CH:2 * CH]
            if wb == 0 and u == 0:
                m_rhs = k.mask_by_block[:, 0:CH] if isinstance(n, int) and n % BPS == 0 else m_rhs
                if not isinstance(n, int):
                    m_rhs = k.mask_by_block[:, bass.ds((n % BPS) * (CH // 2), CH)]
            nc.tensor.matmul(bank[4 + wb][:, :], ident_bf[:, :], m_rhs, start=True, stop=True)
            for w2 in range(2):
                for hp in range(HP):
                    w = 2 * wb + w2
                    ins = nc.tensor.matmul(
                        bank[4 + wb][64 * w2:64 * w2 + 64, hp * DH:(hp + 1) * DH],
                        q_z[:, u, hp, w, :, :].rearrange("p a b -> p (a b)"),
                        k_t[:, u, hp, w * WIN:(w + 2) * WIN], start=False, stop=True,
                        skip_group_check=True)
        ins.then_inc(S["sim_done"], 1)

    def act_scores(act, g, n, u):
        act.wait_ge(S["tr_done"], g * 5 + 11)
        act.wait_ge(S["c_done"], g * 7 + 6)
        nc.scalar.activation(x_keys[:, u, :, :], bank[2 + u][:, :].rearrange("p (w d) -> p w d", w=4),
                             ACT.Copy).then_inc(S["tr_evac"], 1)
        act.wait_ge(S["sim_done"], g + 1)
        for j in range(4):
            act.wait_ge(S["tr_done"], g * 5 + 12 + j)
            src = bank[2 + (u + 1 + j) % 2]
            hp = 4 * (j % 2)
            if j < 2:
                for r in range(2):
                    ins = nc.scalar.activation(
                        q_z[64 * r:64 * r + 64, u, hp:hp + 4, :, r, :],
                        src[64 * r:64 * r + 64, :].rearrange("p (h w q) -> p h w q", h=4, w=4), ACT.Copy)
            else:
                ins = nc.scalar.activation(k_t[:, u, hp:hp + 4, WIN:WIN + BLK],
                                           src[:, :].rearrange("p (h t) -> p h t", h=4), ACT.Copy)
            ins.then_inc(S["tr_evac"], 1)

    def pool_tail(pool, g, n, u):
        pool.wait_ge(S["tr_evac"], g * 5 + 7)
        pool.wait_ge(S["sim_done"], g + 2)
        nc.gpsimd.tensor_tensor(k_t[:, 1 - u, :, 0:WIN], k_t[:, u, :, BLK:BLK + WIN],
                                k.has_next[:, bass.ds(n % BPS, 1)].unsqueeze(2).broadcast_to([P, HP, WIN]),
                                ALU.mult).then_inc(S["tail_ready"], 1)

    def dve_max(dve, g, n, u):
        dve.wait_ge(S["sim_done"], g + 3)
        ch = Chain(dve, S["sm_link"], g * 2)
        ch.link(nc.vector.tensor_reduce(row_max[:, :], k.scores[:, :].rearrange("p (h j) -> p h j", j=DH), AX, ALU.max))
        dve.wait_ge(S["c_done"], g * 7 + 2)
        nc.vector.tensor_tensor(prob[:, u, :, :].rearrange("p b (h j) -> p (b h) j", j=DH),
                                k.scores[:, :].rearrange("p (h j) -> p h j", j=DH),
                                row_max[:, :].unsqueeze(2).broadcast_to([P, 16, DH]),
                                ALU.subtract).then_inc(S["sub_ready"], 1)

    def act_exp(act, g, n, u):
        act.wait_ge(S["sub_ready"], g + 2)
        nc.scalar.activation(prob[:, u, :, :], prob[:, u, :, :], ACT.Exp, scale=8.0).then_inc(S["exp_ready"], 1)

    def dve_sum(dve, g, n, u):
        dve.wait_ge(S["exp_ready"], g + 1)
        ch = Chain(dve, S["sm_link"], g * 2 + 1)
        ch.link(nc.vector.tensor_reduce(row_sum[:, :], prob[:, u, :, :].rearrange("p b (h j) -> p (b h) j", j=DH), AX,
                                        ALU.add))
        dve.wait_ge(S["prob_ready"], g + 1)
        nc.vector.reciprocal(row_inv[:, u, :], row_sum[:, :]).then_inc(S["inv_ready"], 1)

    def pool_prob(pool, g, n, u):
        pool.wait_ge(S["inv_ready"], g + 1)
        pr = prob[:, u, :, :].rearrange("p b (h j) -> p (b h) j", j=DH)
        nc.gpsimd.tensor_tensor(pr, pr, row_inv[:, u, :].unsqueeze(2).broadcast_to([P, 16, DH]),
                                ALU.mult).then_inc(S["prob_ready"], 1)

    def c_bank(u, j):
        return bank[6 + (u + j) % 2]

    def pe_values(pe, g, n, u):
        base = g * 7
        pe.wait_ge(S["prob_ready"], g + 3)
        for wb in range(2):
            pe.wait_ge(S["c_evac"], base + wb + 1)
            for m in range(4):
                ins = nc.tensor.transpose(c_bank(u, wb)[:, m * P:(m + 1) * P],
                                          prob[:, u, wb, m * P:(m + 1) * P], ident[:, :])
            ins.then_inc(S["c_done"], 1)
        pe.wait_ge(S["tr_evac"], g * 5 + 3)
        for j in range(4):
            hpl, wb = j // 2, j % 2
            pe.wait_ge(S["c_evac"], base + 2 + j + 1)
            for w2 in range(2):
                ins = nc.tensor.matmul(
                    c_bank(u, 2 + j)[:, w2 * 256:(w2 + 1) * 256],
                    x_keys[64 * hpl:64 * hpl + 64, u, 2 * wb + w2, :],
                    prob_t[64 * hpl:64 * hpl + 64, wb, :, 64 * w2:64 * w2 + 64], start=True, stop=True)
            ins.then_inc(S["c_done"], 1)
        for i in range(HEADS):
            if i == 0:
                pe.wait_ge(S["c_evac"], base + 7)
            if i == HP:
                pe.wait_ge(S["c_evac"], base + 8)
            hpl, hpp, h2 = i // 8, (i % 8) // 2, i % 2
            ins = nc.tensor.matmul(c_bank(u, 6)[:, 0:BLK], w_vo[:, HP * h2 + 2 * hpp + hpl, :], y_t[:, i, :],
                                   start=(i == 0), stop=(i == HEADS - 1))
        ins.then_inc(S["c_done"], 1)

    def act_values(act, g, n, u):
        base = g * 7 + 14
        for wb in range(2):
            act.wait_ge(S["c_done"], base + wb + 1)
            nc.scalar.activation(prob_t[:, wb, :, :], c_bank(u, wb)[:, :].rearrange("p (h c) -> p h c", h=4),
                                 ACT.Copy).then_inc(S["c_evac"], 1)
        for j in range(4):
            hpl, wb = j // 2, j % 2
            act.wait_ge(S["c_done"], base + 2 + j + 1)
            for w2 in range(2):
                w = 2 * wb + w2
                ins = nc.scalar.activation(
                    y_t[:, 8 * hpl:8 * hpl + 8, w * WIN:(w + 1) * WIN],
                    c_bank(u, 2 + j)[:, w2 * 256:(w2 + 1) * 256].rearrange("p (h q) -> p h q", q=WIN), ACT.Copy)
            ins.then_inc(S["c_evac"], 1)
        act.wait_ge(S["c_done"], base + 7)
        act.wait_ge(S["xb_ready"], g + 1)
        nc.scalar.activation(o_t[:, u, :], c_bank(u, 6)[:, 0:BLK], ACT.Copy).then_inc(S["c_evac"], 1)

    def pool_residual(pool, g, n, u):
        pool.wait_ge(S["c_evac"], g * 7 + 9)
        at = bass.ds(blk_off(n), BLK)
        nc.gpsimd.tensor_tensor(x_b[:, at], x_a[:, at], o_t[:, u, :], ALU.add).then_inc(S["xb_ready"], 1)

    STEPS = {
        "tensor": [(pe_project, 0), (pe_values, 3), (pe_scores, 1)],
        "scalar": [(act_exp, 2), (act_project, 0), (act_values, 3), (act_scores, 1)],
        "vector": [(dve_max, 2), (dve_rope, 0), (dve_sum, 2)],
        "gpsimd": [(pool_rope, 0), (pool_prob, 2), (pool_shift, -1), (pool_residual, 3), (pool_tail, 1)],
    }

    def attention(eng, steps, layer):
        def step(m, u, low, high):
            for f, lag in steps:
                if low <= lag <= high:
                    f(eng, layer * NBLK + (m - lag), m - lag, (u - lag) % 2)

        if any(lag < 0 for _, lag in steps):
            step(-1, 1, -1, -1)
        for m in range(4):
            step(m, m % 2, -1, m)
        with eng.Fori(2, NBLK // 2 - 1) as pair:
            for u in range(2):
                step(pair * 2 + u, u, -1, 3)
        for m in range(NBLK - 2, NBLK + 3):
            step(m, m % 2, m - NBLK + 1, 3)


    def pool_ffn_shift(pool, q, c, u):
        pool.wait_ge(S["f_cen"], q + 1)
        ch = Chain(pool, S["f_shift_link"], q)
        k.settle(pool)
        ch.link(nc.gpsimd.tensor_copy(xf[0:64, u, :], x_b[0:64, bass.ds(chunk_off(c), CH)]))
        k.settle(pool)
        nc.gpsimd.tensor_copy(xf[64:128, u, :], x_b[64:128, bass.ds(chunk_off(c) - 1, CH)]).then_inc(S["f_xs"], 1)
        pool.wait_ge(S["f_xs"], q + 1)
        k.settle(pool)

    def pe_ffn_centre(pe, q, c, u):
        pe.wait_ge(S["f_xs"], q + 1)
        pe.wait_ge(S["f_xn"], q + 1)
        nc.tensor.matmul(bank[0][:, :], k.centre[:, :], xf[:, u, :], start=True, stop=True).then_inc(S["f_cen"], 1)

    def pe_ffn_var(pe, q, c, u):
        pe.wait_ge(S["f_sq"], q + 1)
        pe.wait_ge(S["f_std"], q + 1)
        nc.tensor.matmul(bank[1][:, :], k.mean[:, :], k.nsq[:, 0, :], start=True, stop=True).then_inc(S["f_var"], 1)

    def pe_ffn_up(pe, q, c, u):
        pe.wait_ge(S["f_xn"], q + 2)
        for j, (r, m) in enumerate(FIT):
            pe.wait_ge(S["f_gate"], q * 3 + j + 1)
            nc.tensor.matmul(bank[2 + (u + j) % 2][0:m, :], w1[:, FI + r:FI + r + m], xn[:, u, :],
                             start=True, stop=True).then_inc(S["f_gate_mm"], 1)
            pe.wait_ge(S["f_hid"], q * 3 + j + 1)
            nc.tensor.matmul(bank[4 + (u + j) % 2][0:m, :], w1[:, r:r + m], xn[:, u, :],
                             start=True, stop=True).then_inc(S["f_a_mm"], 1)

    def pe_ffn_down(pe, q, c, u):
        pe.wait_ge(S["xa_ready"], q + 1)
        for j, (r, m) in enumerate(FIT):
            pe.wait_ge(S["f_hid"], q * 3 + j + 3)
            ins = nc.tensor.matmul(bank[6 + u][:, :], w2[0:m, j, :], hid[0:m, j, :], start=(j == 0), stop=(j == 2))
        ins.then_inc(S["f_out_mm"], 1)

    def act_ffn_square(act, q, c, u):
        act.wait_ge(S["f_cen"], q + 3)
        act.wait_ge(S["f_var"], q + 1)
        nc.scalar.activation(k.nsq[:, 0, :], bank[0][:, :], ACT.Square).then_inc(S["f_sq"], 1)

    def act_ffn_gate(act, q, c, u):
        for j, (r, m) in enumerate(FIT):
            act.wait_ge(S["f_gate_mm"], q * 3 + j + 1)
            act.wait_ge(S["f_hid"], q * 3 + j + 1)
            nc.scalar.activation(gate[0:m, (u + j) % 2, :], bank[2 + (u + j) % 2][0:m, :], ACT.Gelu,
                                 bias=fvec[0:m, 6 + j:7 + j]).then_inc(S["f_gate"], 1)

    def act_ffn_std(act, q, c, u):
        act.wait_ge(S["f_var"], q + 2)
        act.wait_ge(S["f_xn"], q + 1)
        nc.scalar.activation(k.nstd[:, 0, :], bank[1][:, :], ACT.Sqrt, bias=k.eps[:, 0:1]).then_inc(S["f_std"], 1)

    def dve_ffn_hidden(dve, q, c, u):
        dve.wait_ge(S["f_out_mm"], q + 1)
        for j, (r, m) in enumerate(FIT):
            dve.wait_ge(S["f_gate"], q * 3 + j + 3)
            dve.wait_ge(S["f_a_mm"], q * 3 + j + 1)
            nc.vector.scalar_tensor_tensor(out=hid[0:m, j, :], in0=bank[4 + (u + j) % 2][0:m, :],
                                           scalar=fvec[0:m, 3 + j:4 + j], in1=gate[0:m, (u + j) % 2, :],
                                           op0=ALU.add, op1=ALU.mult).then_inc(S["f_hid"], 1)

    def dve_ffn_norm(dve, q, c, u):
        dve.wait_ge(S["f_std"], q + 2)
        ch = Chain(dve, S["f_link"], q * 2)
        ch.link(nc.vector.reciprocal(k.nrs[:, 0, :], k.nstd[:, 0, :]))
        ch.link(nc.vector.tensor_tensor(k.nrs[:, 0, :], bank[0][:, :], k.nrs[:, 0, :], ALU.mult))
        nc.vector.tensor_scalar(xn[:, u, :], k.nrs[:, 0, :], fvec[:, 0:1], fvec[:, 1:2], ALU.mult,
                                ALU.add).then_inc(S["f_xn"], 1)

    def dve_ffn_out(dve, q, c, u):
        dve.wait_ge(S["f_out_mm"], q + 2)
        at = bass.ds(chunk_off(c), CH)
        nc.vector.scalar_tensor_tensor(out=x_a[:, at], in0=bank[6 + u][:, :], scalar=fvec[:, 2:3], in1=x_b[:, at],
                                       op0=ALU.add, op1=ALU.add).then_inc(S["xa_ready"], 1)

    FSTEPS = {
        "tensor": [(pe_ffn_centre, -1), (pe_ffn_up, 0), (pe_ffn_var, -1), (pe_ffn_down, 0)],
        "scalar": [(act_ffn_square, -1), (act_ffn_gate, 0), (act_ffn_std, -1)],
        "vector": [(dve_ffn_hidden, 0), (dve_ffn_norm, -1), (dve_ffn_out, 0)],
        "gpsimd": [(pool_ffn_shift, -1)],
    }

    def ffn(eng, steps, layer):
        def step(m, u, low, high):
            for f, lag in steps:
                if low <= lag <= high:
                    f(eng, layer * NCH + (m - lag), m - lag, (u - lag) % 2)

        step(-1, 1, -1, -1)
        with eng.Fori(0, NCH // 2 - 1) as pair:
            for u in range(2):
                step(pair * 2 + u, u, -1, 0)
        step(NCH - 2, 0, -1, 0)
        step(NCH - 1, 1, 0, 0)


    def sync(sp):
        sp.dma_start(k.mask_by_block[:, :].bitcast(U16), dram["mask_tab"]).then_inc(S["const_loaded"], 16)
        sp.dma_start(ident_bf[:, :].bitcast(U16), dram["ident_bf"]).then_inc(S["const_loaded"], 16)

        def load(layer):
            sp.dma_start(w_qk[:, :], dram["w_qk"][bass.ds(layer * P, P), :]).then_inc(S["qk_loaded"], 16)

        def load_vo(layer):
            sp.dma_start(wv_t[:, :, :], dram["wv_t"][bass.ds(layer * P, P), :, :]).then_inc(S["vo_loaded"], 16)
            sp.dma_start(w_o[:, :, :], dram["w_o"][bass.ds(layer * P, P), :, :]).then_inc(S["vo_loaded"], 16)

        def load_scale(layer):
            sp.dma_start(rot[:, :, :], dram["rot_tab"]).then_inc(S["scale_loaded"], 16)
            sp.dma_start(rot_scale[:, :], dram["rot_scale"][bass.ds(layer, 1), :].broadcast_to([P, 256])
                         ).then_inc(S["scale_loaded"], 16)

        def load_ffn(layer):
            sp.dma_start(w1[:, :], dram["w1"][bass.ds(layer * P, P), :]).then_inc(S["ffn_loaded"], 16)
            sp.dma_start(w2[:, :, :], dram["w2"][bass.ds(layer * P, P), :, :]).then_inc(S["ffn_loaded"], 16)
            sp.dma_start(fvec[:, :], dram["fvec"][bass.ds(layer * P, P), :]).then_inc(S["ffn_loaded"], 16)

        load_vo(0)
        load_scale(0)
        load(0)
        load_ffn(0)
        with sp.Fori(0, DEPTH - 1) as layer:
            sp.wait_ge(S["vo_done"], layer * 4 + 4)
            load_vo(layer + 1)
            sp.wait_ge(S["proj_done"], layer * 4 * NBLK + 4 * NBLK)
            load(layer + 1)
            sp.wait_ge(S["rope_ready"], layer * NBLK + NBLK + 2)
            load_scale(layer + 1)
            sp.wait_ge(S["xa_ready"], layer * NCH + NCH + 2)
            load_ffn(layer + 1)

    FFN_DMAS = 3

    def tensor(pe):
        pe.sem_inc(S["tr_done"], 10)
        pe.sem_inc(S["c_done"], 14)
        pe.sem_inc(S["sim_done"], 2)
        pe.sem_inc(S["f_cen"], 2)
        pe.sem_inc(S["f_var"], 1)
        pe.sem_inc(S["f_out_mm"], 1)
        pe.wait_ge(k.N["n_out"], (norm_index + 1) * NCH + 2)
        pe.wait_ge(S["const_loaded"], 32)
        with pe.Fori(0, DEPTH) as layer:
            pe.wait_ge(S["vo_loaded"], layer * 32 + 32)
            pe.wait_ge(S["xa_ready"], layer * NCH + 2)
            for j in range(4):
                for m in range(4):
                    r, hp = 64 * (j // 2), 4 * (j % 2) + m
                    ins = nc.tensor.matmul(bank[j][:, m * D:(m + 1) * D], wv_t[r:r + 64, hp, :],
                                           w_o[r:r + 64, hp, :], start=True, stop=True)
                ins.then_inc(S["vo_done"], 1)
            pe.wait_ge(S["vo_evac"], layer * 4 + 4)
            pe.wait_ge(S["qk_loaded"], layer * 16 + 16)
            attention(pe, STEPS["tensor"], layer)
            pe.wait_ge(S["ffn_loaded"], layer * 16 * FFN_DMAS + 16 * FFN_DMAS)
            pe.wait_ge(S["c_evac"], layer * 7 * NBLK + 7 * NBLK + 2)
            ffn(pe, FSTEPS["tensor"], layer)

    def scalar(act):
        act.sem_inc(S["proj_evac"], 2)
        act.sem_inc(S["tr_evac"], 2)
        act.sem_inc(S["c_evac"], 2)
        act.sem_inc(S["f_gate"], 2)
        act.sem_inc(S["f_std"], 1)
        act.wait_ge(S["layer_init"], 5)
        with act.Fori(0, DEPTH) as layer:
            for j in range(4):
                act.wait_ge(S["vo_done"], layer * 4 + j + 1)
                nc.scalar.activation(w_vo[:, 4 * j:4 * j + 4, :], bank[j][:, :].rearrange("p (h d) -> p h d", h=4),
                                     ACT.Copy).then_inc(S["vo_evac"], 1)
            attention(act, STEPS["scalar"], layer)
            act.wait_ge(S["ffn_loaded"], layer * 16 * FFN_DMAS + 16 * FFN_DMAS)
            ffn(act, FSTEPS["scalar"], layer)

    def vector(dve):
        dve.sem_inc(S["sq_summed"], 1)
        dve.sem_inc(S["rot_link"], 2)
        dve.sem_inc(S["rope_ready"], 2)
        dve.sem_inc(S["sub_ready"], 1)
        dve.sem_inc(S["f_xn"], 1)
        dve.sem_inc(S["f_hid"], 2)
        dve.sem_inc(S["xa_ready"], 2)
        with dve.Fori(0, DEPTH) as layer:
            dve.wait_ge(S["rot_ready"], layer + 1)
            attention(dve, STEPS["vector"], layer)
            dve.wait_ge(S["ffn_loaded"], layer * 16 * FFN_DMAS + 16 * FFN_DMAS)
            dve.wait_ge(S["xb_ready"], layer * NBLK + NBLK + 2)
            ffn(dve, FSTEPS["vector"], layer)

    def gpsimd(pool):
        nc.gpsimd.memset(k.has_next[:, 0:BPS - 1], 1.0).then_inc(S["layer_init"], 1)
        nc.gpsimd.memset(k.has_next[:, BPS - 1:BPS], 0.0).then_inc(S["layer_init"], 1)
        pool.sem_inc(S["tail_ready"], 1)
        pool.sem_inc(S["prob_ready"], 2)
        pool.sem_inc(S["xb_ready"], 2)
        nc.gpsimd.memset(minus_half[:, :], -0.5).then_inc(S["layer_init"], 1)
        nc.gpsimd.memset(k_t[:, 0, :, 0:WIN], 0.0).then_inc(S["layer_init"], 1)
        nc.gpsimd.memset(q_z[:, :, :, :, :, :], 0.0).then_inc(S["layer_init"], 1)
        pool.wait_ge(S["layer_init"], 5)
        pool.wait_ge(k.N["n_out"], (norm_index + 1) * NCH + 2)
        pool.wait_ge(S["const_loaded"], 32)
        with pool.Fori(0, DEPTH) as layer:
            pool.wait_ge(S["scale_loaded"], layer * 32 + 32)
            nc.gpsimd.tensor_tensor(rot[:, :, :], rot[:, :, :],
                                    rot_scale[:, :].unsqueeze(1).broadcast_to([P, BPS, 256]),
                                    ALU.mult).then_inc(S["rot_ready"], 1)
            pool.wait_ge(S["rot_ready"], layer + 1)
            pool.wait_ge(S["xa_ready"], layer * NCH + 2)
            k.settle(pool)
            attention(pool, STEPS["gpsimd"], layer)
            pool.wait_ge(S["xb_ready"], layer * NBLK + NBLK + 2)
            k.settle(pool)
            ffn(pool, FSTEPS["gpsimd"], layer)

    k.layers_done = (S["xa_ready"], DEPTH * NCH + 2)
    return {"sync": sync, "tensor": tensor, "scalar": scalar, "vector": vector, "gpsimd": gpsimd}

def after(k, part, done):
    def waiting(program):
        def run(eng):
            if done:
                eng.wait_ge(*done)
            program(eng)
        return run

    return {name: waiting(program) for name, program in part.items()}


def early_stages(nc, k, dram, stages):
    parts, n, last = [], 0, None
    for name, stage in (("A", ssm_stage), ("B", moe_stage), ("C", conv_stage)):
        if name not in stages:
            continue
        with ExitStack() as k.stage:
            parts.append(norm_pass(nc, k, n, k.x_in, k.x_a))
            k.norm_index = n
            parts.append(after(k, stage(nc, k, dram), last))
            last = k.stage_done
            parts.append(norm_pass(nc, k, n + 1, k.x_b, k.x_in, res=k.x_in, ready=k.stage_done))
        n += 2
    return parts, n



def build(nc, dram, out, stages="ABCD"):
    ctx = ExitStack()
    with ctx:
        k = Parts(nc, ctx)
        k.norm_links = 0
        k.stage_done = None
        k.ident = k.sb("ident", [P, P])
        k.centre = k.sb("centre", [P, P])
        k.mean = k.sb("mean", [P, P])
        k.eps = k.sb("eps", [P, 1])
        k.x_in = k.sb("x_in", [P, XW])
        k.x_a = k.sb("x_a", [P, XW])
        k.x_b = k.sb("x_b", [P, XW])
        psum = ctx.enter_context(nc.psum_tensor("banks", [P, 8 * CH], F32))
        k.bank = [psum[:, i * CH:(i + 1) * CH] for i in range(8)]
        k.bank_bf = [b.bitcast(BF16) for b in k.bank]
        k.scores = psum[:, 4 * CH:6 * CH]
        norm_parts(nc, k)
        G = k.sems("shared_loaded input_loaded zeros_made stored settled")
        k.settle = lambda eng: eng.sem_inc(G["settled"], 1)
        x_in, x_a, x_b = k.x_in, k.x_a, k.x_b

        parts = []
        npass = 0
        consts = (G["shared_loaded"], 64)
        if "A" in stages or "B" in stages or "C" in stages:
            parts, npass = early_stages(nc, k, dram, stages)
        if "D" in stages:
            with ExitStack() as k.stage:
                first = norm_pass(nc, k, npass, x_in, x_a, ready=(G["input_loaded"], 16 * NSEQ) if npass == 0 else None)
                k.has_next = k.sb("has_next", [P, BPS])
                k.mask_by_block = k.sb("mask_by_block", [P, BPS // 2 * CH], BF16)
                layers = after(k, layers_stage(nc, k, dram, npass), k.stage_done)
                last = norm_pass(nc, k, npass + 1, x_a, x_in, res=x_in, ready=k.layers_done)
                parts += [first, layers, last]
            npass += 2
        presets = norm_presets(nc, k)
        block = ctx.enter_context(nc.Block())

        def run(eng, name):
            for s, v in presets.get(name, []):
                eng.sem_inc(s, v)
            eng.wait_ge(*consts)
            eng.wait_ge(G["input_loaded"], 16 * NSEQ)
            eng.wait_ge(G["zeros_made"], 4)
            for part in parts:
                if name in part:
                    part[name](eng)

        @block.sync
        def _(sp):
            for dst, src in ((k.ident, "ident"), (k.centre, "centre"), (k.mean, "mean"), (k.eps, "eps")):
                sp.dma_start(dst[:, :], dram[src]).then_inc(G["shared_loaded"], 16)
            for s in range(NSEQ):
                at = s * SEQW + PAD
                sp.dma_start(x_in[:, at:at + SLEN], dram["x"][:, s * SLEN:(s + 1) * SLEN]
                             ).then_inc(G["input_loaded"], 16)
            for part in parts:
                if "sync" in part:
                    part["sync"](sp)
            sp.wait_ge(k.N["n_out"], npass * NCH + 2)
            for s in range(NSEQ):
                at = s * SEQW + PAD
                sp.dma_start(out[:, s * SLEN:(s + 1) * SLEN], x_in[:, at:at + SLEN]).then_inc(G["stored"], 16)
            sp.wait_ge(G["stored"], 16 * NSEQ)

        @block.tensor
        def _(pe):
            run(pe, "tensor")

        @block.scalar
        def _(act):
            run(act, "scalar")

        @block.vector
        def _(dve):
            for x in (x_a, x_b):
                for s in range(2):
                    nc.vector.memset(x[:, :].rearrange("p (s c) -> p s c", s=NSEQ)[:, 2 * s:2 * s + 2, 0:PAD],
                                     0.0).then_inc(G["zeros_made"], 1)
            run(dve, "vector")

        @block.gpsimd
        def _(pool):
            run(pool, "gpsimd")


def constants():
    import numpy as np
    f = np.float32
    half = np.arange(0, DH, 2, dtype=f)
    inv_freq = (1.0 / f(10000.0) ** (half / DH)).astype(f)
    t = np.arange(SLEN, dtype=f)
    freqs = t[:, None] * inv_freq[None, :]
    freqs = np.concatenate([freqs, freqs], -1).astype(f)
    base = ((half + f(0.4 * DH)) / f(1.4 * DH)).astype(f)
    power = (t - SLEN // 2) / f(WIN // 2)
    scale = (base[None, :] ** power[:, None]).astype(f)
    scale = np.concatenate([scale, scale], -1)
    inv = f(1.0) / scale
    sign = np.concatenate([-np.ones(DH // 2, f), np.ones(DH // 2, f)])
    rows = np.concatenate([np.cos(freqs) * scale, np.cos(freqs) * inv, np.sin(freqs) * scale * sign,
                           np.sin(freqs) * inv * sign], -1).astype(f)
    rot_tab = rows.reshape(BPS, BLK, 256).transpose(1, 0, 2)
    w2, h2, q, j = np.meshgrid(np.arange(2), np.arange(2), np.arange(WIN), np.arange(2 * WIN), indexing="ij")
    usual = np.where((q <= j) & (j <= q + WIN), 0.0, MASKED).reshape(P, 2 * WIN)
    first = np.where((q <= j) & (j <= q + WIN) & ((w2 == 1) | (j >= WIN)), 0.0, MASKED).reshape(P, 2 * WIN)
    usual, first = (np.tile(m, (1, HP)) for m in (usual, first))

    def bf16(a):
        return (np.ascontiguousarray(a, f).view(np.uint32) >> 16).astype(np.uint16)

    pick = np.zeros((3, 2 * N_ST, 2 * N_ST, P), f)
    pick[:, np.arange(2 * N_ST), np.arange(2 * N_ST), :] = 1
    spread = np.zeros((3, 2, HEADS, 2, HEADS, D // HEADS), f)
    for i in range(2):
        for hd in range(HEADS):
            spread[:, i, hd, i, hd, :] = 1
    spread = spread.reshape(96, 2, P)
    pick8 = pick[:, :EXPERTS, :EXPERTS].reshape(3 * EXPERTS, EXPERTS, P)
    pick = pick.reshape(96, 2 * N_ST, P)
    return {
        "ident": np.eye(P, dtype=f), "centre": (np.eye(P) - 1.0 / P).astype(f),
        "mean": np.full((P, P), 1.0 / P, f), "eps": np.full((P, 1), EPS, f),
        "rot_tab": np.ascontiguousarray(rot_tab), "ident_bf": bf16(np.eye(P)),
        "pick": bf16(pick), "spread": bf16(spread), "pick8": bf16(pick8),
        "rank": np.ascontiguousarray(np.broadcast_to(EXPERTS - np.arange(EXPERTS, dtype=f), (P, TB, EXPERTS))),
        "mask_tab": bf16(np.concatenate([first] + [usual] * (BPS // 2 - 1), 1)),
    }


def layouts(a):
    import numpy as np
    c = np.ascontiguousarray
    w = a["L1_ffn_Wqkv"]
    wv = w[:, :, 2 * INNER:].reshape(DEPTH, D, HP, 2 * DH)
    qs, ks = a["L1_ffn_q_scale"], a["L1_ffn_k_scale"]
    r = DH // 2
    tail = 3 * P - FI
    w2 = np.pad(a["L1_ffn_W2"], ((0, 0), (0, tail), (0, 0)))
    b1 = np.pad(a["L1_ffn_b1"].reshape(DEPTH, 2, FI), ((0, 0), (0, 0), (0, tail))).reshape(DEPTH, 6, P)
    w_x = a["L0_attn_W_x"]
    bc = w_x[DT_RANK:].T
    out = {
        "wx_dt": c(w_x[:DT_RANK].T), "wx_bc": c(np.concatenate([bc, bc, bc], 1)), "w_dt": c(a["L0_attn_W_dt"].T),
        "avec": c(np.concatenate([a["L0_attn_A_log"], a["L0_attn_b_dt"][:, None], a["L0_attn_D_param"][:, None]], 1)),
        "w_router": c(a["L0_ffn_w_router"].T), "w_up": c(a["L0_ffn_w_up"].transpose(2, 0, 1)),
        "w_dn": c(a["L0_ffn_w_down"].reshape(EXPERTS, D, UT, P).transpose(3, 0, 2, 1)),
        "evec": c(np.concatenate([a["L0_ffn_b_up"].reshape(EXPERTS, UT, P), a["L0_ffn_b_down"][:, None, :]], 1)
                  .transpose(2, 0, 1)),
        "w_lin": c(a["L1_attn_w_lin"].reshape(HEADS, TAPS, D).transpose(2, 1, 0).reshape(D, TAPS * HEADS)),
        "x": c(a["L0_attn_u"].reshape(T, D).T),
        "w_qk": c(w[:, :, :2 * INNER].reshape(DEPTH * D, 2 * INNER)),
        "wv_t": c(wv.transpose(0, 3, 2, 1).reshape(DEPTH * P, HP, D)),
        "w_o": c(a["L1_ffn_Wo"].reshape(DEPTH, HP, 2 * DH, D).transpose(0, 2, 1, 3).reshape(DEPTH * P, HP, D)),
        "rot_scale": c(np.concatenate([qs, ks, np.roll(qs, r, -1), np.roll(ks, r, -1)], -1)),
        "w1": c(a["L1_ffn_W1"].reshape(DEPTH * D, 2 * FI)),
        "w2": c(w2.reshape(DEPTH, 3, P, D).transpose(0, 2, 1, 3).reshape(DEPTH * P, 3, D)),
        "fvec": c(np.stack([a["L1_ffn_ln_g"], a["L1_ffn_ln_b"], a["L1_ffn_b2"], *b1.transpose(1, 0, 2)],
                           -1).reshape(DEPTH * D, 9)),
    }
    return out


def kernel(**inputs):
    import numpy as np
    import concourse.bacc as bacc
    from concourse.bass_utils import run_bass_kernel_spmd

    arrays = {**constants(), **layouts({n: np.asarray(v) for n, v in inputs.items()})}
    nc = bacc.Bacc("TRN2", target_bir_lowering=False, num_devices=1)
    dram = {n: nc.dram_tensor("in_" + n, a.shape, mybir.dt.from_np(a.dtype), kind="ExternalInput").ap()
            for n, a in arrays.items()}
    out = nc.dram_tensor("out_t", (D, T), F32, kind="ExternalOutput").ap()
    build(nc, dram, out)
    r = run_bass_kernel_spmd(nc, [{"in_" + n: a for n, a in arrays.items()}], core_ids=[0])
    return np.ascontiguousarray(r.results[0]["out_t"].T).reshape(NSEQ, SLEN, D)
```

```python
from contextlib import ExitStack

import concourse.bass as bass
from concourse import mybir
from concourse.alu_op_type import AluOpType as ALU

F32 = mybir.dt.float32
BF16 = mybir.dt.bfloat16
U16 = mybir.dt.uint16
ACT = mybir.ActivationFunctionType
AX = mybir.AxisListType.X

P = 128
D = 128
NSEQ, SLEN = 4, 1024
T = NSEQ * SLEN
PAD = 36
SEQW = PAD + SLEN
XW = NSEQ * SEQW
CH = 512
NCH = T // CH
QPC = CH // P
CPS = SLEN // CH
EPS = 1e-5

MASKED = -1e37
BLK = 128
NBLK = T // BLK
BPS = SLEN // BLK
WIN = 32
HEADS, DH = 16, 64
HP = HEADS // 2
DEPTH = 6
INNER = HEADS * DH
FI = 341
FIT = [(0, P), (P, P), (2 * P, FI - 2 * P)]


def blk_off(n):
    return n * BLK + (n // BPS) * PAD + PAD


def chunk_off(c):
    return c * CH + (c // CPS) * PAD + PAD


class Chain:

    def __init__(self, eng, sem, base):
        self.eng, self.sem, self.count = eng, sem, base

    def link(self, ins):
        self.count = self.count + 1
        ins.then_inc(self.sem, 1)
        self.eng.wait_ge(self.sem, self.count)


class Parts:

    def __init__(self, nc, ctx):
        self.nc, self.ctx, self.stage = nc, ctx, ctx

    def sb(self, name, shape, dt=F32):
        return self.stage.enter_context(self.nc.sbuf_tensor(name, shape, dt))

    def sems(self, names):
        return {n: self.ctx.enter_context(self.nc.semaphore(n)) for n in names.split()}




def norm_parts(nc, k):
    k.norm_buf = k.sb("norm_buf", [P, 6 * CH])
    k.nsq, k.ncen, k.nrs = (k.norm_buf[:, 2 * i * CH:2 * (i + 1) * CH].rearrange("p (u t) -> p u t", u=2)
                            for i in range(3))
    k.nstd = k.sb("nstd", [P, QPC])
    k.ninv = k.sb("ninv", [P, 2, QPC])
    k.N = k.sems("n_cen n_sq n_var n_std n_inv n_bc n_copy n_link n_out")


def norm_presets(nc, k):
    return {"tensor": [(k.N["n_var"], 2)], "scalar": [(k.N["n_copy"], 2)], "vector": [(k.N["n_out"], 2), (k.N["n_inv"], 1)]}


def variance(nc, k, bank, squares):
    for q in range(QPC):
        ins = nc.tensor.matmul(bank[:, q:q + 1], squares[:, q * P:(q + 1) * P], k.mean[:, 0:1], start=True, stop=True)
    return ins


def spread_inverse(nc, k, bank, u):
    for q in range(QPC):
        ins = nc.tensor.matmul(bank[:, q * P:(q + 1) * P], k.ninv[:, u, q:q + 1].broadcast_to([P, P]),
                               k.ident[:, :], start=True, stop=True)
    return ins


def norm_pass(nc, k, index, src, dst, res=None, ready=None):
    N, bank = k.N, k.bank

    def loop(eng, step):
        step(eng, 0, 0)
        with eng.Fori(0, NCH // 2 - 1) as p:
            for u in (1, 0):
                step(eng, p * 2 + (1 if u else 2), u)
        step(eng, NCH - 1, 1)

    def pe_step(pe, c, u):
        pe.wait_ge(N["n_copy"], index * NCH + c + 1)
        nc.tensor.matmul(bank[u][:, :], k.centre[:, :], src[:, bass.ds(chunk_off(c), CH)],
                         start=True, stop=True).then_inc(N["n_cen"], 1)
        if not isinstance(c, int) or c > 0:
            pe_spread(pe, c - 1, 1 - u)
        pe.wait_ge(N["n_sq"], index * NCH + c + 1)
        pe.wait_ge(N["n_out"], index * NCH + c + 1)
        variance(nc, k, bank[2 + u], k.nsq[:, u, :]).then_inc(N["n_var"], 1)

    def pe_spread(pe, c, u):
        pe.wait_ge(N["n_inv"], index * NCH + c + 2)
        spread_inverse(nc, k, bank[2 + u], u).then_inc(N["n_bc"], 1)

    def tensor(pe):
        if ready:
            pe.wait_ge(*ready)
        loop(pe, pe_step)
        pe_spread(pe, NCH - 1, 1)

    def act_step(act, c, u):
        act.wait_ge(N["n_cen"], index * NCH + c + 1)
        act.wait_ge(N["n_var"], index * NCH + c + 1)
        nc.scalar.activation(k.nsq[:, u, :], bank[u][:, :], ACT.Square).then_inc(N["n_sq"], 1)
        act.wait_ge(N["n_out"], index * NCH + c + 1)
        nc.scalar.activation(k.ncen[:, u, :], bank[u][:, :], ACT.Copy).then_inc(N["n_copy"], 1)
        act.wait_ge(N["n_var"], index * NCH + c + 3)
        act.wait_ge(N["n_inv"], index * NCH + c + 1)
        nc.scalar.activation(k.nstd[:, :], bank[2 + u][:, 0:QPC], ACT.Sqrt, bias=k.eps[:, 0:1]).then_inc(N["n_std"], 1)

    def scalar(act):
        loop(act, act_step)

    def dve_scale(dve, c, u):
        dve.wait_ge(N["n_copy"], index * NCH + c + 3)
        dve.wait_ge(N["n_bc"], index * NCH + c + 1)
        out = dst[:, bass.ds(chunk_off(c), CH)]
        if res is None:
            nc.vector.tensor_tensor(out, bank[2 + u][:, :], k.ncen[:, u, :], ALU.mult).then_inc(N["n_out"], 1)
        else:
            ch = Chain(dve, N["n_link"], k.norm_links + c)
            ch.link(nc.vector.tensor_tensor(k.nrs[:, u, :], bank[2 + u][:, :], k.ncen[:, u, :], ALU.mult))
            nc.vector.tensor_tensor(out, k.nrs[:, u, :], res[:, bass.ds(chunk_off(c), CH)],
                                    ALU.add).then_inc(N["n_out"], 1)

    def vector(dve):
        def step(dve, c, u):
            if not isinstance(c, int) or c > 0:
                dve_scale(dve, c - 1, 1 - u)
            dve.wait_ge(N["n_std"], index * NCH + c + 1)
            nc.vector.reciprocal(k.ninv[:, u, :], k.nstd[:, :]).then_inc(N["n_inv"], 1)

        loop(dve, step)
        dve_scale(dve, NCH - 1, 1)
        k.norm_links += NCH if res is not None else 0

    return {"tensor": tensor, "scalar": scalar, "vector": vector}


N_ST = 16
DT_RANK = 64
LOG1P_TERMS = 7


def ssm_stage(nc, k, dram):
    bank, x_a, x_b = k.bank, k.x_a, k.x_b
    sb = k.sb
    wx_dt = sb("wx_dt", [P, DT_RANK])
    wx_bc = sb("wx_bc", [P, 96])
    w_dt = sb("w_dt", [DT_RANK, D])
    avec = sb("avec", [P, N_ST + 2])
    a_neg = sb("a_neg", [P, N_ST])
    pick = sb("pick", [96, 2 * N_ST, P], BF16)
    dt = sb("dt", [P, T])
    dtu = sb("dtu", [P, T])
    bc3 = sb("bc3", [96, T], BF16)
    raw = sb("raw", [DT_RANK, CH])
    e_abs = sb("e_abs", [P, 2, CH])
    relu = sb("relu", [P, 2, CH])
    tmp = sb("tmp", [P, 3, CH])
    rest = sb("rest", [96, CH])
    a_bar = sb("a_bar", [P, 2, SLEN])
    b_rep = sb("b_rep", [P, 2, SLEN])
    dbu = sb("dbu", [P, 2, SLEN])
    h = sb("h", [P, 2, SLEN])
    hc = sb("hc", [P, 2, SLEN])
    S = k.sems("""a_loaded a_exp a_ready a_raw_mm a_raw a_dt_mm a_abs a_eabs a_relu a_bc_mm a_hi a_r1 a_mid a_r2 a_lo
        a_link a_q a_dt a_dtu a_b_mm a_b a_abar a_dbu a_c_mm a_scan a_hc a_y_mm a_out""")

    base = k.norm_index * NCH

    def sync(sp):
        for dst, src in ((wx_dt[:, :], "wx_dt"), (wx_bc[:, :], "wx_bc"), (w_dt[:, :], "w_dt"), (avec[:, :], "avec"),
                         (pick[:, :, :].bitcast(U16), "pick")):
            sp.dma_start(dst, dram[src]).then_inc(S["a_loaded"], 16)


    def tensor(pe):
        pe.wait_ge(S["a_loaded"], 80)
        pe.sem_inc(S["a_y_mm"], 2)
        pe.sem_inc(S["a_dt_mm"], 1)
        with pe.Fori(0, NCH) as c:
            pe.wait_ge(k.N["n_out"], base + c + 3)
            u = x_a[:, bass.ds(chunk_off(c), CH)]
            pe.wait_ge(S["a_raw"], c + 1)
            nc.tensor.matmul(bank[5][0:DT_RANK, :], wx_dt[:, :], u, start=True, stop=True).then_inc(S["a_raw_mm"], 1)
            pe.wait_ge(S["a_r1"], c + 1)
            nc.tensor.matmul(bank[4][0:96, :], wx_bc[:, :], u, start=True, stop=True).then_inc(S["a_bc_mm"], 1)
            pe.wait_ge(S["a_raw"], c + 2)
            pe.wait_ge(S["a_relu"], c + 1)
            nc.tensor.matmul(bank[6][:, :], w_dt[:, :], raw[:, :], start=True, stop=True).then_inc(S["a_dt_mm"], 1)
        pe.wait_ge(S["a_lo"], NCH)
        pe.wait_ge(S["a_relu"], NCH + 1)
        pe.wait_ge(S["a_r1"], NCH + 1)
        with pe.Fori(0, NSEQ) as s:
            def y_mm(n):
                for half in range(2):
                    pe.wait_ge(S["a_hc"], s * 32 + (2 * n + half + 3))
                    ins = nc.tensor.matmul(bank[2 + half][:, :], k.ident[:, :],
                                           hc[:, n % 2, half * CH:(half + 1) * CH], start=(n == 0),
                                           stop=(n == N_ST - 1))
                ins.then_inc(S["a_y_mm"], 1)

            for n in range(N_ST):
                for half in range(2):
                    rows = bc3[:, bass.ds(s * SLEN + half * CH, CH)]
                    pe.wait_ge(S["a_b"], s * 32 + (2 * n + half + 1))
                    nc.tensor.matmul(bank[4 + half][:, :], pick[:, n, :], rows, start=True,
                                     stop=True).then_inc(S["a_b_mm"], 1)
                for half in range(2):
                    rows = bc3[:, bass.ds(s * SLEN + half * CH, CH)]
                    pe.wait_ge(S["a_hc"], s * 32 + (2 * n + half + 1))
                    nc.tensor.matmul(bank[6 + half][:, :], pick[:, N_ST + n, :], rows, start=True,
                                     stop=True).then_inc(S["a_c_mm"], 1)
                if n == 1:
                    pe.wait_ge(S["a_out"], s * 2 + 1)
                if n >= 1:
                    y_mm(n - 1)
            y_mm(N_ST - 1)

    def scalar(act):
        act.sem_inc(S["a_raw"], 1)
        act.sem_inc(S["a_relu"], 1)
        act.sem_inc(S["a_b"], 2)
        act.wait_ge(S["a_loaded"], 80)
        nc.scalar.activation(a_neg[:, :], avec[:, 0:N_ST], ACT.Exp).then_inc(S["a_exp"], 1)
        with act.Fori(0, NCH // 2) as pair:
            for u in range(2):
                c = pair * 2 + u
                act.wait_ge(S["a_raw_mm"], c + 1)
                act.wait_ge(S["a_dt_mm"], c + 1)
                nc.scalar.activation(raw[:, :], bank[5][0:DT_RANK, :], ACT.Copy).then_inc(S["a_raw"], 1)
                at = bass.ds(c * CH, CH)
                act.wait_ge(S["a_bc_mm"], c + 1)
                k.settle(act)
                nc.scalar.activation(bc3[:, at], bank[4][0:96, :], ACT.Copy).then_inc(S["a_hi"], 1)
                act.wait_ge(S["a_dt_mm"], c + 2)
                act.wait_ge(S["a_dt"], c + 1)
                nc.scalar.activation(e_abs[:, u, :], bank[6][:, :], ACT.Abs,
                                     bias=avec[:, N_ST:N_ST + 1]).then_inc(S["a_abs"], 1)
                nc.scalar.activation(relu[:, u, :], bank[6][:, :], ACT.Relu,
                                     bias=avec[:, N_ST:N_ST + 1]).then_inc(S["a_relu"], 1)
                act.wait_ge(S["a_abs"], c + 1)
                nc.scalar.activation(e_abs[:, u, :], e_abs[:, u, :], ACT.Exp, scale=-1.0).then_inc(S["a_eabs"], 1)
                act.wait_ge(S["a_r1"], c + 2)
                k.settle(act)
                nc.scalar.activation(bc3[32:64, at], rest[32:64, :], ACT.Copy)
                nc.scalar.activation(bc3[64:96, at], rest[64:96, :], ACT.Copy).then_inc(S["a_mid"], 1)
                act.wait_ge(S["a_r2"], c + 1)
                k.settle(act)
                nc.scalar.activation(bc3[64:96, at], rest[64:96, :], ACT.Copy).then_inc(S["a_lo"], 1)
        act.wait_ge(S["a_dt"], NCH + 2)
        act.wait_ge(S["a_ready"], 1)
        with act.Fori(0, NSEQ) as s:
            for n in range(N_ST):
                for half in range(2):
                    act.wait_ge(S["a_b_mm"], s * 32 + (2 * n + half + 1))
                    if half == 0:
                        act.wait_ge(S["a_dbu"], s * N_ST + (n + 1))
                    nc.scalar.activation(b_rep[:, n % 2, half * CH:(half + 1) * CH], bank[4 + half][:, :],
                                         ACT.Copy).then_inc(S["a_b"], 1)
                act.wait_ge(S["a_scan"], s * N_ST + (n + 1))
                k.settle(act)
                nc.scalar.activation(a_bar[:, n % 2, :], dt[:, bass.ds(s * SLEN, SLEN)], ACT.Exp,
                                     scale=a_neg[:, n:n + 1]).then_inc(S["a_abar"], 1)

    def vector(dve):
        dve.sem_inc(S["a_r1"], 1)
        dve.sem_inc(S["a_dt"], 2)
        dve.sem_inc(S["a_scan"], 2)
        dve.sem_inc(S["a_hc"], 2)
        dve.sem_inc(S["a_out"], 1)
        dve.wait_ge(S["a_exp"], 1)
        nc.vector.tensor_scalar(a_neg[:, :], a_neg[:, :], -1.0, None, ALU.mult).then_inc(S["a_ready"], 1)
        links = LOG1P_TERMS + 4
        with dve.Fori(0, NCH // 2) as pair:
            for u in range(2):
                c = pair * 2 + u
                at = bass.ds(c * CH, CH)
                dve.wait_ge(S["a_hi"], c + 1)
                nc.vector.tensor_tensor(rest[:, :], bank[4][0:96, :], bc3[:, at], ALU.subtract).then_inc(S["a_r1"], 1)
                dve.wait_ge(S["a_eabs"], c + 1)
                ch = Chain(dve, S["a_link"], c * links)
                s1, s2, q = tmp[:, 0, :], tmp[:, 1, :], tmp[:, 2, :]
                ch.link(nc.vector.tensor_scalar(s1, e_abs[:, u, :], 2.0, None, ALU.add))
                ch.link(nc.vector.reciprocal(s2, s1))
                dve.wait_ge(S["a_mid"], c + 1)
                nc.vector.tensor_tensor(rest[64:96, :], rest[64:96, :], bc3[64:96, at],
                                        ALU.subtract).then_inc(S["a_r2"], 1)
                ch.link(nc.vector.tensor_tensor(s1, s2, e_abs[:, u, :], ALU.mult))
                ch.link(nc.vector.tensor_tensor(s2, s1, s1, ALU.mult))
                ch.link(nc.vector.tensor_scalar(q, s2, 1.0 / (2 * LOG1P_TERMS + 1), None, ALU.mult))
                for i in range(LOG1P_TERMS - 1, 0, -1):
                    ch.link(nc.vector.scalar_tensor_tensor(out=q, in0=q, scalar=1.0 / (2 * i + 1), in1=s2, op0=ALU.add,
                                                           op1=ALU.mult))
                nc.vector.scalar_tensor_tensor(out=q, in0=q, scalar=1.0, in1=s1, op0=ALU.add,
                                               op1=ALU.mult).then_inc(S["a_q"], 1)
                dve.wait_ge(S["a_q"], c + 1)
                dve.wait_ge(S["a_relu"], c + 2)
                nc.vector.scalar_tensor_tensor(out=dt[:, at], in0=q, scalar=2.0, in1=relu[:, u, :], op0=ALU.mult,
                                               op1=ALU.add).then_inc(S["a_dt"], 1)
        with dve.Fori(0, NSEQ) as s:
            for n in range(N_ST):
                i = s * N_ST + n
                dve.wait_ge(S["a_abar"], i + 1)
                dve.wait_ge(S["a_dbu"], i + 3)
                nc.vector.tensor_tensor_scan(h[:, n % 2, :], a_bar[:, n % 2, :], dbu[:, n % 2, :], 0.0, ALU.mult,
                                             ALU.add).then_inc(S["a_scan"], 1)
                dve.wait_ge(S["a_scan"], i + 3)
                dve.wait_ge(S["a_y_mm"], i + 1)
                for half in range(2):
                    at = slice(half * CH, (half + 1) * CH)
                    dve.wait_ge(S["a_c_mm"], s * 32 + (2 * n + half + 1))
                    nc.vector.tensor_tensor(hc[:, n % 2, at], h[:, n % 2, at], bank[6 + half][:, :],
                                            ALU.mult).then_inc(S["a_hc"], 1)
            dve.wait_ge(S["a_y_mm"], s * N_ST + N_ST + 2)
            for half in range(2):
                at = bass.ds(s * SEQW + PAD + half * CH, CH)
                nc.vector.scalar_tensor_tensor(out=x_b[:, at], in0=x_a[:, at], scalar=avec[:, N_ST + 1:N_ST + 2],
                                               in1=bank[2 + half][:, :], op0=ALU.mult,
                                               op1=ALU.add).then_inc(S["a_out"], 1)

    def gpsimd(pool):
        pool.sem_inc(S["a_dbu"], 2)
        with pool.Fori(0, NCH) as c:
            pool.wait_ge(S["a_dt"], c + 3)
            k.settle(pool)
            nc.gpsimd.tensor_tensor(dtu[:, bass.ds(c * CH, CH)], dt[:, bass.ds(c * CH, CH)],
                                    x_a[:, bass.ds(chunk_off(c), CH)], ALU.mult).then_inc(S["a_dtu"], 1)
        pool.wait_ge(S["a_dtu"], NCH)
        with pool.Fori(0, NSEQ) as s:
            for n in range(N_ST):
                pool.wait_ge(S["a_b"], s * 32 + (2 * n + 4))
                pool.wait_ge(S["a_scan"], s * N_ST + (n + 1))
                k.settle(pool)
                nc.gpsimd.tensor_tensor(dbu[:, n % 2, :], dtu[:, bass.ds(s * SLEN, SLEN)], b_rep[:, n % 2, :],
                                        ALU.mult).then_inc(S["a_dbu"], 1)

    k.stage_done = (S["a_out"], 2 * NSEQ + 1)
    return {"sync": sync, "tensor": tensor, "scalar": scalar, "vector": vector, "gpsimd": gpsimd}


EXPERTS = 8
FU = 512
UT = FU // P
TB = T // P


def moe_stage(nc, k, dram):
    bank, x_a, x_b, ident = k.bank, k.x_a, k.x_b, k.ident
    sb = k.sb
    w_r = sb("w_router", [P, EXPERTS])
    w_up = sb("w_up", [P, EXPERTS, FU])
    w_dn = sb("w_dn", [P, EXPERTS, UT, D])
    evec = sb("evec", [P, EXPERTS, UT + 1])
    rank = sb("rank", [P, TB, EXPERTS])
    pick8 = sb("pick8", [3 * EXPERTS, EXPERTS, P], BF16)
    logit_t = sb("logit_t", [EXPERTS, 2, CH])
    logits = sb("logits", [P, TB, EXPERTS])
    work = sb("work", [P, 4, TB, EXPERTS])
    top = sb("top", [P, 4, TB])
    gate_w = sb("gate_w", [P, TB, EXPERTS])
    gate3 = sb("gate3", [P, TB, 3, EXPERTS], BF16)
    gate_t = sb("gate_t", [3 * EXPERTS, T], BF16)
    ident_bf = sb("moe_ident_bf", [P, P], BF16)
    hid = sb("moe_hid", [P, 2, UT, CH])
    gate_b = sb("gate_b", [P, 2, CH])
    part = sb("part", [P, 2, CH])
    acc = sb("acc", [P, 2, CH])
    S = k.sems("""b_loaded b_logit_mm b_logit_t b_logit_tr b_logits b_link b_exp b_gate_w b_rest b_gates b_gate_tr b_gate_t
        b_up_mm b_hid b_dn_mm b_gate_mm b_gate b_part b_acc""")
    base = k.norm_index * NCH
    trf = k.bank_bf

    def sync(sp):
        for dst, src in ((w_r[:, :], "w_router"), (w_up[:, :, :], "w_up"), (w_dn[:, :, :, :], "w_dn"),
                         (evec[:, :, :], "evec"), (rank[:, :, :], "rank"), (pick8[:, :, :].bitcast(U16), "pick8"),
                         (ident_bf[:, :].bitcast(U16), "ident_bf")):
            sp.dma_start(dst, dram[src]).then_inc(S["b_loaded"], 16)

    def tensor(pe):
        pe.sem_inc(S["b_logit_mm"], 1)
        pe.sem_inc(S["b_logit_tr"], 1)
        pe.sem_inc(S["b_dn_mm"], 2)
        pe.wait_ge(S["b_loaded"], 112)
        with pe.Fori(0, NCH) as c:
            pe.wait_ge(k.N["n_out"], base + c + 3)
            pe.wait_ge(S["b_logit_t"], c + 1)
            nc.tensor.matmul(bank[4][0:EXPERTS, :], w_r[:, :], x_a[:, bass.ds(chunk_off(c), CH)], start=True,
                             stop=True).then_inc(S["b_logit_mm"], 1)
            pe.wait_ge(S["b_logit_t"], c + 2)
            pe.wait_ge(S["b_logits"], c + 1)
            k.settle(pe)
            for j in range(CH // P):
                ins = nc.tensor.transpose(bank[5][:, j * EXPERTS:(j + 1) * EXPERTS],
                                          logit_t[:, 0, j * P:(j + 1) * P], ident[0:EXPERTS, 0:EXPERTS])
            ins.then_inc(S["b_logit_tr"], 1)
        pe.wait_ge(S["b_gates"], 3)
        for b in range(TB):
            ins = nc.tensor.transpose(trf[4 + b // 8][0:3 * EXPERTS, (b % 8) * P:(b % 8 + 1) * P],
                                      gate3[:, b, :, :].rearrange("p a e -> p (a e)"), ident_bf[:, :])
            if b % 8 == 7:
                ins.then_inc(S["b_gate_tr"], 1)
        pe.wait_ge(S["b_gate_t"], 4)

        def down(c, e):
            i = c * EXPERTS + e
            pe.wait_ge(S["b_part"], i + 1)
            for j in range(UT):
                pe.wait_ge(S["b_hid"], i * UT + (j + 5))
                ins = nc.tensor.matmul(bank[4 + e % 2][:, :], w_dn[:, e, j, :], hid[:, e % 2, j, :], start=(j == 0),
                                       stop=(j == UT - 1))
            ins.then_inc(S["b_dn_mm"], 1)

        with pe.Fori(0, NCH) as c:
            for e in range(EXPERTS):
                i = c * EXPERTS + e
                for j in range(UT):
                    pe.wait_ge(S["b_hid"], i * UT + (j + 1))
                    nc.tensor.matmul(bank[j][:, :], w_up[:, e, j * P:(j + 1) * P],
                                     x_a[:, bass.ds(chunk_off(c), CH)], start=True,
                                     stop=True).then_inc(S["b_up_mm"], 1)
                pe.wait_ge(S["b_gate"], i + 1)
                k.settle(pe)
                nc.tensor.matmul(bank[6 + e % 2][:, :], pick8[:, e, :], gate_t[:, bass.ds(c * CH, CH)], start=True,
                                 stop=True).then_inc(S["b_gate_mm"], 1)
                if e >= 1:
                    down(c, e - 1)
            down(c, EXPERTS - 1)

    def scalar(act):
        act.sem_inc(S["b_logit_t"], 1)
        act.sem_inc(S["b_logits"], 1)
        act.sem_inc(S["b_hid"], 4)
        act.sem_inc(S["b_gate"], 2)
        act.wait_ge(S["b_loaded"], 112)
        with act.Fori(0, NCH) as c:
            act.wait_ge(S["b_logit_mm"], c + 2)
            act.wait_ge(S["b_logit_tr"], c + 1)
            nc.scalar.activation(logit_t[:, 0, :], bank[4][0:EXPERTS, :], ACT.Copy).then_inc(S["b_logit_t"], 1)
            act.wait_ge(S["b_logit_tr"], c + 2)
            k.settle(act)
            nc.scalar.activation(logits[:, bass.ds(c * (CH // P), CH // P), :],
                                 bank[5][:, 0:CH // P * EXPERTS].rearrange("p (b e) -> p b e", e=EXPERTS),
                                 ACT.Copy).then_inc(S["b_logits"], 1)
        act.wait_ge(S["b_link"], 9)
        nc.scalar.activation(top[:, 2, :], top[:, 2, :], ACT.Exp).then_inc(S["b_exp"], 1)
        act.wait_ge(S["b_gate_w"], 1)
        nc.scalar.activation(gate3[:, :, 0, :], gate_w[:, :, :], ACT.Copy).then_inc(S["b_gates"], 1)
        act.wait_ge(S["b_rest"], 1)
        nc.scalar.activation(gate3[:, :, 1, :], work[:, 0, :, :], ACT.Copy).then_inc(S["b_gates"], 1)
        act.wait_ge(S["b_rest"], 2)
        nc.scalar.activation(gate3[:, :, 2, :], work[:, 1, :, :], ACT.Copy).then_inc(S["b_gates"], 1)
        for q in range(4):
            act.wait_ge(S["b_gate_tr"], q + 1)
            nc.scalar.activation(gate_t[:, q * 8 * P:(q + 1) * 8 * P], trf[4 + q][0:3 * EXPERTS, 0:8 * P],
                                 ACT.Copy).then_inc(S["b_gate_t"], 1)
        with act.Fori(0, NCH) as c:
            for e in range(EXPERTS):
                i = c * EXPERTS + e
                act.wait_ge(S["b_dn_mm"], i + 1)
                for j in range(UT):
                    act.wait_ge(S["b_up_mm"], i * UT + (j + 1))
                    nc.scalar.activation(hid[:, e % 2, j, :], bank[j][:, :], ACT.Gelu,
                                         bias=evec[:, e, j:j + 1]).then_inc(S["b_hid"], 1)
                act.wait_ge(S["b_gate_mm"], i + 1)
                act.wait_ge(S["b_part"], i + 1)
                nc.scalar.activation(gate_b[:, e % 2, :], bank[6 + e % 2][:, :], ACT.Copy).then_inc(S["b_gate"], 1)

    def vector(dve):
        dve.sem_inc(S["b_part"], 2)
        dve.wait_ge(S["b_logits"], NCH + 1)
        dve.wait_ge(S["b_loaded"], 112)
        ch = Chain(dve, S["b_link"], 0)

        def one_of(src, hot, best):
            ch.link(nc.vector.tensor_reduce(best, src, AX, ALU.max))
            ch.link(nc.vector.tensor_tensor(hot, src, best.unsqueeze(2).broadcast_to([P, TB, EXPERTS]), ALU.is_equal))
            ch.link(nc.vector.tensor_tensor(hot, hot, rank[:, :, :], ALU.mult))
            ch.link(nc.vector.tensor_reduce(top[:, 3, :], hot, AX, ALU.max))

        wide = lambda a: a.unsqueeze(2).broadcast_to([P, TB, EXPERTS])
        hot1, hot2, rest = work[:, 0, :, :], work[:, 1, :, :], work[:, 2, :, :]
        one_of(logits[:, :, :], hot1, top[:, 0, :])
        ch.link(nc.vector.tensor_tensor(hot1, rank[:, :, :], wide(top[:, 3, :]), ALU.is_equal))
        ch.link(nc.vector.scalar_tensor_tensor(out=rest, in0=hot1, scalar=-3e38, in1=logits[:, :, :], op0=ALU.mult,
                                               op1=ALU.add))
        ch.link(nc.vector.tensor_reduce(top[:, 1, :], rest, AX, ALU.max))
        ch.link(nc.vector.tensor_tensor(hot2, rest, wide(top[:, 1, :]), ALU.is_equal))
        ch.link(nc.vector.tensor_tensor(top[:, 2, :], top[:, 1, :], top[:, 0, :], ALU.subtract))
        ch.link(nc.vector.tensor_tensor(hot2, hot2, rank[:, :, :], ALU.mult))
        ch.link(nc.vector.tensor_reduce(top[:, 3, :], hot2, AX, ALU.max))
        ch.link(nc.vector.tensor_tensor(hot2, rank[:, :, :], wide(top[:, 3, :]), ALU.is_equal))
        dve.wait_ge(S["b_exp"], 1)
        ch.link(nc.vector.tensor_scalar(top[:, 0, :], top[:, 2, :], 1.0, None, ALU.add))
        ch.link(nc.vector.reciprocal(top[:, 1, :], top[:, 0, :]))
        ch.link(nc.vector.tensor_tensor(top[:, 2, :], top[:, 2, :], top[:, 1, :], ALU.mult))
        ch.link(nc.vector.tensor_tensor(hot1, hot1, wide(top[:, 1, :]), ALU.mult))
        ch.link(nc.vector.tensor_tensor(hot2, hot2, wide(top[:, 2, :]), ALU.mult))
        nc.vector.tensor_tensor(gate_w[:, :, :], hot1, hot2, ALU.add).then_inc(S["b_gate_w"], 1)
        dve.wait_ge(S["b_gates"], 1)
        nc.vector.tensor_tensor(work[:, 0, :, :], gate_w[:, :, :], gate3[:, :, 0, :], ALU.subtract).then_inc(S["b_rest"], 1)
        dve.wait_ge(S["b_rest"], 1)
        dve.wait_ge(S["b_gates"], 2)
        nc.vector.tensor_tensor(work[:, 1, :, :], work[:, 0, :, :], gate3[:, :, 1, :],
                                ALU.subtract).then_inc(S["b_rest"], 1)
        with dve.Fori(0, NCH) as c:
            for e in range(EXPERTS):
                i = c * EXPERTS + e
                dve.wait_ge(S["b_dn_mm"], i + 3)
                dve.wait_ge(S["b_gate"], i + 3)
                dve.wait_ge(S["b_acc"], i + 1)
                nc.vector.scalar_tensor_tensor(out=part[:, e % 2, :], in0=bank[4 + e % 2][:, :],
                                               scalar=evec[:, e, UT:UT + 1], in1=gate_b[:, e % 2, :], op0=ALU.add,
                                               op1=ALU.mult).then_inc(S["b_part"], 1)

    def gpsimd(pool):
        pool.sem_inc(S["b_acc"], 2)
        with pool.Fori(0, NCH) as c:
            for e in range(EXPERTS):
                i = c * EXPERTS + e
                if e == 0:
                    continue
                pool.wait_ge(S["b_part"], i + 3)
                if e > 1:
                    pool.wait_ge(S["b_acc"], i + 2)
                first = part[:, 0, :] if e == 1 else acc[:, (e - 1) % 2, :]
                out = x_b[:, bass.ds(chunk_off(c), CH)] if e == EXPERTS - 1 else acc[:, e % 2, :]
                if e == EXPERTS - 1:
                    k.settle(pool)
                ins = nc.gpsimd.tensor_tensor(out, first, part[:, e % 2, :], ALU.add)
                ins.then_inc(S["b_acc"], 2 if e == 1 else 1)

    k.stage_done = (S["b_acc"], EXPERTS * NCH + 2)
    return {"sync": sync, "tensor": tensor, "scalar": scalar, "vector": vector, "gpsimd": gpsimd}


TAPS = 31
WCOLS = 512
WG = WCOLS // 32
PE_ADDS = (TAPS + 1) // 2
POOL_ADDS = TAPS // 2
CB = CH // P
FIRST_TURN = 12


def conv_stage(nc, k, dram):
    bank, x_a, x_b = k.bank, k.x_a, k.x_b
    sb = k.sb
    w_lin = sb("w_lin", [P, TAPS * HEADS])
    spread = sb("spread", [96, 2, P], BF16)
    ident_bf = sb("conv_ident_bf", [P, P], BF16)
    xc = sb("xc", [P, 2, CH])
    w = sb("conv_w", [P, CB, WCOLS])
    w_rest = sb("conv_rest", [P, CB, WCOLS])
    w3 = sb("conv_w3", [P, CB, WG, 3, 32], BF16)
    w_t = sb("conv_wt", [96, 2, WG, CH], BF16)
    mx = sb("conv_max", [P, CB, HEADS])
    sm = sb("conv_sum", [P, CB, HEADS])
    inv = sb("conv_inv", [P, CB, HEADS])
    pe_prod = sb("pe_prod", [P, 2, CH])
    pool_prod = sb("pool_prod", [P, 2, CH])
    acc = sb("conv_acc", [P, CH])
    S = k.sems("""v_loaded v_zero v_xc v_log_mm v_link v_sub v_exp v_norm v_hi v_r1 v_mid v_r2 v_lo v_tr v_wt
        v_tap_mm v_prod v_add_mm v_add v_out""")
    base = k.norm_index * NCH
    by_head = lambda a: a.rearrange("p (k h) -> p h k", h=HEADS)
    by_group = lambda a: a.rearrange("p (g i) -> p g i", g=WG)
    LIVE = TAPS * HEADS

    def sync(sp):
        for dst, src in ((w_lin[:, :], "w_lin"), (spread[:, :, :].bitcast(U16), "spread"), (ident_bf[:, :].bitcast(U16), "ident_bf")):
            sp.dma_start(dst, dram[src]).then_inc(S["v_loaded"], 16)


    def pool_copy(pool, c, u):
        pool.wait_ge(k.N["n_out"], base + c + 3)
        pool.wait_ge(S["v_log_mm"], c * CB + 4)
        k.settle(pool)
        nc.gpsimd.tensor_copy(xc[:, u, :], x_a[:, bass.ds(chunk_off(c), CH)]).then_inc(S["v_xc"], 1)

    def pe_logits(pe, c, u):
        pe.wait_ge(S["v_xc"], c + 1)
        for b in range(CB):
            pe.wait_ge(S["v_sub"], c * CB + (b + 1))
            nc.tensor.matmul(bank[b % 2][:, 0:LIVE], xc[:, u, b * P:(b + 1) * P], w_lin[:, :], start=True,
                             stop=True).then_inc(S["v_log_mm"], 1)

    def dve_weights(dve, c, u):
        ch = Chain(dve, S["v_link"], c * (3 * CB))
        for b in range(CB):
            dve.wait_ge(S["v_log_mm"], c * CB + (b + 9))
            lo = bank[b % 2][:, 0:LIVE]
            ch.link(nc.vector.tensor_reduce(mx[:, b, :], by_head(lo), AX, ALU.max))
            dve.wait_ge(S["v_r1"], c * CB + (b + 1))
            nc.vector.tensor_tensor(by_head(w[:, b, 0:LIVE]), by_head(lo),
                                    mx[:, b, :].unsqueeze(2).broadcast_to([P, HEADS, TAPS]),
                                    ALU.subtract).then_inc(S["v_sub"], 1)
        for b in range(CB):
            dve.wait_ge(S["v_exp"], c * CB + (b + 1))
            live = by_head(w[:, b, 0:LIVE])
            ch.link(nc.vector.tensor_reduce(sm[:, b, :], live, AX, ALU.add))
            ch.link(nc.vector.reciprocal(inv[:, b, :], sm[:, b, :]))
            nc.vector.tensor_tensor(live, live, inv[:, b, :].unsqueeze(2).broadcast_to([P, HEADS, TAPS]),
                                    ALU.mult).then_inc(S["v_norm"], 1)

    def act_weights(act, c, u):
        for b in range(CB):
            act.wait_ge(S["v_sub"], c * CB + (b + 3))
            nc.scalar.activation(w[:, b, 0:LIVE], w[:, b, 0:LIVE], ACT.Exp).then_inc(S["v_exp"], 1)
        for part, ready, lag, done in ((0, "v_norm", 1, "v_hi"), (1, "v_r1", 5, "v_mid"), (2, "v_r2", 1, "v_lo")):
            for b in range(CB):
                act.wait_ge(S[ready], c * CB + (b + lag))
                if part == 0:
                    act.wait_ge(S["v_tr"], c * 2 * CB + (2 * b + 2))
                src = (w if part == 0 else w_rest)[:, b, :]
                nc.scalar.activation(w3[:, b, :, part, :], by_group(src), ACT.Copy).then_inc(S[done], 1)

    def pool_rest(pool, c, u, i):
        b = i % CB
        if i < CB:
            pool.wait_ge(S["v_hi"], c * CB + (b + 1))
            pool.wait_ge(S["v_lo"], c * CB + (b + 1))
            nc.gpsimd.tensor_tensor(by_group(w_rest[:, b, :]), by_group(w[:, b, :]), w3[:, b, :, 0, :],
                                    ALU.subtract).then_inc(S["v_r1"], 1)
        else:
            pool.wait_ge(S["v_mid"], c * CB + (b + 1))
            nc.gpsimd.tensor_tensor(by_group(w_rest[:, b, :]), by_group(w_rest[:, b, :]), w3[:, b, :, 1, :],
                                    ALU.subtract).then_inc(S["v_r2"], 1)

    def pe_turn(pe, c, u, j):
        b, half = j // 2, j % 2
        pe.wait_ge(S["v_lo"], c * CB + (b + 5))
        pe.wait_ge(S["v_wt"], c * 2 * CB + (j + 1))
        for g in range(WG // 2):
            ins = nc.tensor.transpose(k.bank_bf[2 + half][0:96, g * P:(g + 1) * P],
                                      w3[:, b, half * (WG // 2) + g, :, :].rearrange("p a i -> p (a i)"),
                                      ident_bf[:, :])
        ins.then_inc(S["v_tr"], 1)

    def act_turn(act, c, u):
        act.wait_ge(S["v_tap_mm"], c * TAPS + TAPS)
        for j in range(2 * CB):
            b, half = j // 2, j % 2
            act.wait_ge(S["v_tr"], c * 2 * CB + (j + 9))
            nc.scalar.activation(w_t[:, u, half * (WG // 2):(half + 1) * (WG // 2), b * P:(b + 1) * P],
                                 k.bank_bf[2 + half][0:96, :].rearrange("p (g t) -> p g t", t=P),
                                 ACT.Copy).then_inc(S["v_wt"], 1)


    def pe_add(pe, c, u, tap):
        pe.wait_ge(S["v_prod"], c * TAPS + (tap + 3))
        if tap == 0:
            pe.wait_ge(S["v_out"], c + 1)
        nc.tensor.matmul(bank[7][:, :], k.ident[:, :], pe_prod[:, (tap // 2) % 2, :], start=(tap == 0),
                         stop=(tap == TAPS - 1)).then_inc(S["v_add_mm"], 1)

    def pe_taps(pe, c, u, more):
        pe.wait_ge(S["v_wt"], c * 2 * CB + (2 * CB + 2))
        for tap in range(TAPS):
            pe.wait_ge(S["v_prod"], c * TAPS + (tap + 1))
            nc.tensor.matmul(bank[4 + (u + tap) % 2][:, :], spread[:, tap % 2, :], w_t[:, u, tap // 2, :], start=True,
                             stop=True).then_inc(S["v_tap_mm"], 1)
            if tap >= 2 and tap % 2 == 0:
                pe_add(pe, c, u, tap - 2)
            if more and tap >= FIRST_TURN and tap % 2 == 0 and tap < FIRST_TURN + 4 * CB:
                pe_turn(pe, c + 1, 1 - u, (tap - FIRST_TURN) // 2)
        pe_add(pe, c, u, TAPS - 1)

    def dve_taps(dve, c, u):
        for tap in range(TAPS):
            dve.wait_ge(S["v_tap_mm"], c * TAPS + (tap + 1 + 2 * TAPS))
            if tap % 2 == 0:
                dve.wait_ge(S["v_add_mm"], c * PE_ADDS + (tap // 2 + 1))
                out = pe_prod[:, (tap // 2) % 2, :]
            else:
                dve.wait_ge(S["v_add"], c * POOL_ADDS + (tap // 2 + 1))
                out = pool_prod[:, (u + tap // 2) % 2, :]
            x = x_a[:, bass.ds(chunk_off(c) + tap - (TAPS - 1), CH)]
            nc.vector.tensor_tensor(out, x, bank[4 + (u + tap) % 2][:, :], ALU.mult).then_inc(S["v_prod"], 1)
        dve.wait_ge(S["v_add_mm"], c * PE_ADDS + (PE_ADDS + 2))
        dve.wait_ge(S["v_add"], c * POOL_ADDS + (POOL_ADDS + 2))
        nc.vector.tensor_tensor(x_b[:, bass.ds(chunk_off(c), CH)], acc[:, :], bank[7][:, :],
                                ALU.add).then_inc(S["v_out"], 1)

    def pool_taps(pool, c, u, more):
        for i in range(POOL_ADDS):
            if i > 0:
                pool.wait_ge(S["v_prod"], c * TAPS + (2 * i + 4))
                if i == 1:
                    pool.wait_ge(S["v_out"], c + 1)
                else:
                    pool.wait_ge(S["v_add"], c * POOL_ADDS + (i + 2))
                first = pool_prod[:, u, :] if i == 1 else acc[:, :]
                nc.gpsimd.tensor_tensor(acc[:, :], first, pool_prod[:, (u + i) % 2, :],
                                        ALU.add).then_inc(S["v_add"], 2 if i == 1 else 1)
            if more and i <= CB:
                for r in range(CB) if i == 0 else (CB + i - 1,):
                    pool_rest(pool, c + 1, 1 - u, r)

    def steps(eng, weights, taps):
        weights(eng, 0, 0)
        with eng.Fori(0, NCH // 2 - 1) as pair:
            for u in range(2):
                weights(eng, pair * 2 + (u + 1), 1 - u)
                taps(eng, pair * 2 + u, u, True)
        weights(eng, NCH - 1, 1)
        taps(eng, NCH - 2, 0, True)
        taps(eng, NCH - 1, 1, False)

    def tensor(pe):
        pe.sem_inc(S["v_log_mm"], 8)
        pe.sem_inc(S["v_tr"], 8)
        pe.sem_inc(S["v_tap_mm"], 2 * TAPS)
        pe.sem_inc(S["v_add_mm"], 2)
        pe.wait_ge(S["v_loaded"], 48)
        pe.wait_ge(k.N["n_out"], base + NCH + 2)
        pe_logits(pe, 0, 0)
        for j in range(2 * CB):
            pe_turn(pe, 0, 0, j)
        with pe.Fori(0, NCH // 2 - 1) as pair:
            for u in range(2):
                pe_logits(pe, pair * 2 + (u + 1), 1 - u)
                pe_taps(pe, pair * 2 + u, u, True)
        pe_logits(pe, NCH - 1, 1)
        pe_taps(pe, NCH - 2, 0, True)
        pe_taps(pe, NCH - 1, 1, False)

    def scalar(act):
        act.sem_inc(S["v_lo"], 4)
        act.sem_inc(S["v_wt"], 2)
        act.wait_ge(S["v_zero"], 1)

        def weights(act, c, u):
            act_weights(act, c, u)
            act_turn(act, c, u)

        steps(act, weights, lambda *a: None)

    def vector(dve):
        dve.sem_inc(S["v_sub"], 2)
        dve.sem_inc(S["v_prod"], 2)
        dve.sem_inc(S["v_out"], 1)
        steps(dve, dve_weights, lambda dve, c, u, more: dve_taps(dve, c, u))

    def gpsimd(pool):
        pool.sem_inc(S["v_r1"], 4)
        pool.sem_inc(S["v_add"], 2)
        nc.gpsimd.memset(w[:, :, LIVE:], 0.0).then_inc(S["v_zero"], 1)
        pool.wait_ge(S["v_zero"], 1)
        pool_copy(pool, 0, 0)
        pool_copy(pool, 1, 1)
        for i in range(2 * CB):
            pool_rest(pool, 0, 0, i)
        with pool.Fori(0, NCH // 2 - 1) as pair:
            for u in range(2):
                pool_taps(pool, pair * 2 + u, u, True)
                pool_copy(pool, pair * 2 + (u + 2), u)
        pool_taps(pool, NCH - 2, 0, True)
        pool_taps(pool, NCH - 1, 1, False)

    k.stage_done = (S["v_out"], NCH + 1)
    return {"sync": sync, "tensor": tensor, "scalar": scalar, "vector": vector, "gpsimd": gpsimd}



def layers_stage(nc, k, dram, norm_index):
    bank, x_a, x_b, ident = k.bank, k.x_a, k.x_b, k.ident
    sb = k.sb
    w_qk = sb("w_qk", [P, 2 * INNER])
    wv_t = sb("wv_t", [P, HP, D])
    w_o = sb("w_o", [P, HP, D])
    w_vo = sb("w_vo", [P, HEADS, D])
    rot = sb("rot", [P, BPS, 256])
    rot_scale = sb("rot_scale", [P, 256])
    xs = sb("xs", [P, 2, WIN + BLK])
    xs2 = sb("xs2", [P, 2, 4, 2, 2 * WIN])
    qk_raw = sb("qk_raw", [P, 2, 2 * INNER])
    qk_sq = sb("qk_sq", [P, 2 * INNER])
    rot_b = sb("rot_b", [P, 2 * INNER])
    qk_rot = sb("qk_rot", [P, 2, 2 * INNER])
    norm2 = sb("norm2", [P, 32])
    log_norm2 = sb("log_norm2", [P, 32])
    rnorm = sb("rnorm", [P, 32])
    q_z = sb("q_z", [P, 2, HP, 4, 2, WIN])
    k_t = sb("k_t", [P, 2, HP, WIN + BLK])
    x_keys = sb("x_keys", [P, 2, 4, D])
    prob = sb("prob", [P, 2, 2, CH])
    row_max = sb("row_max", [P, 16])
    row_sum = sb("row_sum", [P, 16])
    row_inv = sb("row_inv", [P, 2, 16])
    prob_t = sb("prob_t", [P, 2, 4, P])
    y_t = k.norm_buf[:, 0:HEADS * BLK].rearrange("p (h t) -> p h t", h=HEADS)
    xf, xn, gate = (qk_rot[:, :, :].rearrange("p a (b t) -> p (a b t)", t=CH)[:, 2 * i * CH:2 * (i + 1) * CH]
                    .rearrange("p (u t) -> p u t", u=2) for i in range(3))
    hid = qk_sq[:, 0:3 * CH].rearrange("p (j t) -> p j t", j=3)
    f_sq, f_cen, f_tmp = qk_sq[:, 3 * CH:4 * CH], rot_b[:, 0:CH], rot_b[:, CH:2 * CH]
    o_t = sb("o_t", [P, 2, BLK])
    ident_bf = sb("ident_bf", [P, P], BF16)
    w1 = sb("w1", [P, 2 * FI])
    w2 = sb("w2", [P, 3, D])
    fvec = sb("fvec", [P, 9])

    S = k.sems("""const_loaded qk_loaded vo_loaded scale_loaded ffn_loaded layer_init
        vo_done vo_evac rot_ready shift_link xs_ready
        proj_done proj_evac sq_done sq_summed ln_ready rn_ready rotb_ready rot_link rotb_used rope_ready
        tr_done tr_evac tail_ready sim_done sub_ready sm_link exp_ready inv_ready prob_ready
        c_done c_evac xb_ready
        f_shift_link f_xs f_cen f_sq f_var f_std f_copy f_inv f_bc f_link f_xn f_gate_mm f_a_mm f_gate f_hid f_out_mm xa_ready""")


    def pool_shift(pool, g, n, u):
        pool.wait_ge(S["tr_done"], g * 5 + 1)
        if isinstance(n, int) and n == 1:
            pool.wait_ge(S["xs_ready"], g)
        elif not isinstance(n, int) or n > 0:
            pool.wait_ge(S["rotb_ready"], g)
        ch = Chain(pool, S["shift_link"], g * 2)
        k.settle(pool)
        ch.link(nc.gpsimd.tensor_copy(xs[0:64, u, :], x_a[0:64, bass.ds(blk_off(n) - WIN, WIN + BLK)]))
        k.settle(pool)
        ch.link(nc.gpsimd.tensor_copy(xs[64:128, u, :], x_a[64:128, bass.ds(blk_off(n) - WIN - 1, WIN + BLK)]))
        k.settle(pool)
        for dup in range(2):
            ins = nc.gpsimd.tensor_copy(xs2[:, u, :, dup, 0:WIN],
                                        xs[:, u, 0:BLK].rearrange("p (w c) -> p w c", w=4))
            ins = nc.gpsimd.tensor_copy(xs2[:, u, :, dup, WIN:2 * WIN],
                                        xs[:, u, WIN:WIN + BLK].rearrange("p (w c) -> p w c", w=4))
        ins.then_inc(S["xs_ready"], 1)

    def pe_project(pe, g, n, u):
        pe.wait_ge(S["xs_ready"], g + 1)
        for j in range(4):
            pe.wait_ge(S["proj_evac"], g * 4 + j + 1)
            nc.tensor.matmul(bank[j % 2][:, :], xs[:, u, WIN:WIN + BLK], w_qk[:, j * CH:(j + 1) * CH],
                             start=True, stop=True).then_inc(S["proj_done"], 1)

    def act_project(act, g, n, u):
        act.wait_ge(S["rope_ready"], g + 1)
        for j in range(4):
            act.wait_ge(S["proj_done"], g * 4 + j + 1)
            nc.scalar.activation(qk_raw[:, u, j * CH:(j + 1) * CH], bank[j % 2][:, :],
                                 ACT.Copy).then_inc(S["proj_evac"], 1)
            if j in (1, 2):
                act_square(act, g, n, u, j - 1)

    def act_square(act, g, n, u, j):
        if j == 0:
            act.wait_ge(S["sq_summed"], g + 1)
        act.wait_ge(S["proj_evac"], g * 4 + j + 3)
        nc.scalar.activation(qk_sq[:, j * CH:(j + 1) * CH], qk_raw[:, u, j * CH:(j + 1) * CH],
                             ACT.Square).then_inc(S["sq_done"], 1)

    def dve_norms(dve, g, n, u):
        dve.wait_ge(S["sq_done"], g * 4 + 4)
        dve.wait_ge(S["rn_ready"], g + 1)
        ch = Chain(dve, S["rot_link"], g * 3 + 3)
        ch.link(nc.vector.tensor_reduce(norm2[:, :], qk_sq[:, :].rearrange("p (h d) -> p h d", d=DH), AX, ALU.add))
        nc.vector.tensor_scalar(norm2[:, :], norm2[:, :], 1e-24, None, ALU.max).then_inc(S["sq_summed"], 1)
        dve.wait_ge(S["tr_done"], g * 5 + 5)
        cos = rot[:, bass.ds(n % BPS, 1), 0:128].rearrange("p o (q d) -> p (o q) d", q=2)
        out = qk_rot[:, u, :].rearrange("p (q h d) -> p q h d", q=2, d=DH)
        ch.link(nc.vector.tensor_tensor(out, qk_raw[:, u, :].rearrange("p (q h d) -> p q h d", q=2, d=DH),
                                        cos.unsqueeze(2).broadcast_to([P, 2, HEADS, DH]), ALU.mult))

    def dve_rope(dve, g, n, u):
        dve.wait_ge(S["rotb_ready"], g + 1)
        nc.vector.tensor_tensor(qk_rot[:, u, :], qk_rot[:, u, :], rot_b[:, :], ALU.add).then_inc(S["rot_link"], 1)

    def dve_scale(dve, g, n, u):
        dve.wait_ge(S["rot_link"], g * 3 + 6)
        dve.wait_ge(S["rn_ready"], g + 2)
        flat = qk_rot[:, u, :].rearrange("p (h d) -> p h d", d=DH)
        nc.vector.tensor_tensor(flat, flat, rnorm[:, :].unsqueeze(2).broadcast_to([P, 32, DH]),
                                ALU.mult).then_inc(S["rope_ready"], 1)

    def act_norms(act, g, n, u):
        act.wait_ge(S["sq_summed"], g + 2)
        nc.scalar.activation(log_norm2[:, :], norm2[:, :], ACT.Ln).then_inc(S["ln_ready"], 1)
        act.wait_ge(S["rope_ready"], g + 2)
        act.wait_ge(S["ln_ready"], g + 1)
        nc.scalar.activation(rnorm[:, :], log_norm2[:, :], ACT.Exp, scale=-0.5).then_inc(S["rn_ready"], 1)

    def pool_rope(pool, g, n, u):
        pool.wait_ge(S["proj_evac"], g * 4 + 6)
        pool.wait_ge(S["rot_link"], g * 3 + 3)
        src = qk_raw[:, u, :].rearrange("p (q h d) -> p q h d", q=2, d=DH)
        dst = rot_b[:, :].rearrange("p (q h d) -> p q h d", q=2, d=DH)
        sin = rot[:, bass.ds(n % BPS, 1), 128:256].rearrange("p o (q d) -> p (o q) d", q=2)
        for d0, s0 in ((0, DH // 2), (DH // 2, 0)):
            for q in range(2):
                ins = nc.gpsimd.tensor_tensor(
                    dst[:, q, :, d0:d0 + DH // 2], src[:, q, :, s0:s0 + DH // 2],
                    sin[:, q:q + 1, d0:d0 + DH // 2].broadcast_to([P, HEADS, DH // 2]), ALU.mult)
        ins.then_inc(S["rotb_ready"], 1)

    def pe_keys(pe, g, n, u):
        pe.wait_ge(S["tr_evac"], g * 5 + 1)
        for w in range(4):
            ins = nc.tensor.transpose(bank[2 + u][:, w * D:(w + 1) * D],
                                      xs2[:, u, w, :, :].rearrange("p a b -> p (a b)"), ident[:, :])
        ins.then_inc(S["tr_done"], 1)

    def pe_heads(pe, g, n, u, j):
        pe.wait_ge(S["rope_ready"], g + 3)
        pe.wait_ge(S["tr_evac"], g * 5 + 2 + j)
        for m in range(4):
            ins = nc.tensor.transpose(bank[2 + (u + 1 + j) % 2][:, m * P:(m + 1) * P],
                                      qk_rot[:, u, (4 * j + m) * P:(4 * j + m + 1) * P], ident[:, :])
        ins.then_inc(S["tr_done"], 1)

    def pe_scores(pe, g, n, u):
        pe.wait_ge(S["sub_ready"], g + 1)
        pe.wait_ge(S["tr_evac"], g * 5 + 7)
        pe.wait_ge(S["tail_ready"], g + 1)
        for wb in range(2):
            m_rhs = k.mask_by_block[:, CH:2 * CH]
            if wb == 0 and u == 0:
                m_rhs = k.mask_by_block[:, 0:CH] if isinstance(n, int) and n % BPS == 0 else m_rhs
                if not isinstance(n, int):
                    m_rhs = k.mask_by_block[:, bass.ds((n % BPS) * (CH // 2), CH)]
            nc.tensor.matmul(bank[4 + wb][:, :], ident_bf[:, :], m_rhs, start=True, stop=True)
            for w2 in range(2):
                for hp in range(HP):
                    w = 2 * wb + w2
                    ins = nc.tensor.matmul(
                        bank[4 + wb][64 * w2:64 * w2 + 64, hp * DH:(hp + 1) * DH],
                        q_z[:, u, hp, w, :, :].rearrange("p a b -> p (a b)"),
                        k_t[:, u, hp, w * WIN:(w + 2) * WIN], start=False, stop=True,
                        skip_group_check=True)
        ins.then_inc(S["sim_done"], 1)

    def act_scores(act, g, n, u):
        act.wait_ge(S["tr_done"], g * 5 + 11)
        act.wait_ge(S["c_done"], g * 7 + 6)
        nc.scalar.activation(x_keys[:, u, :, :], bank[2 + u][:, :].rearrange("p (w d) -> p w d", w=4),
                             ACT.Copy).then_inc(S["tr_evac"], 1)
        act.wait_ge(S["sim_done"], g + 1)
        for j in range(4):
            act.wait_ge(S["tr_done"], g * 5 + 12 + j)
            src = bank[2 + (u + 1 + j) % 2]
            hp = 4 * (j % 2)
            if j < 2:
                for r in range(2):
                    ins = nc.scalar.activation(
                        q_z[64 * r:64 * r + 64, u, hp:hp + 4, :, r, :],
                        src[64 * r:64 * r + 64, :].rearrange("p (h w q) -> p h w q", h=4, w=4), ACT.Copy)
            else:
                ins = nc.scalar.activation(k_t[:, u, hp:hp + 4, WIN:WIN + BLK],
                                           src[:, :].rearrange("p (h t) -> p h t", h=4), ACT.Copy)
            ins.then_inc(S["tr_evac"], 1)

    def pool_tail(pool, g, n, u):
        pool.wait_ge(S["tr_evac"], g * 5 + 7)
        pool.wait_ge(S["sim_done"], g + 2)
        nc.gpsimd.tensor_tensor(k_t[:, 1 - u, :, 0:WIN], k_t[:, u, :, BLK:BLK + WIN],
                                k.has_next[:, bass.ds(n % BPS, 1)].unsqueeze(2).broadcast_to([P, HP, WIN]),
                                ALU.mult).then_inc(S["tail_ready"], 1)

    def dve_max(dve, g, n, u):
        dve.wait_ge(S["sim_done"], g + 3)
        ch = Chain(dve, S["sm_link"], g * 2)
        ch.link(nc.vector.tensor_reduce(row_max[:, :], k.scores[:, :].rearrange("p (h j) -> p h j", j=DH), AX, ALU.max))
        dve.wait_ge(S["c_done"], g * 7 + 2)
        nc.vector.tensor_tensor(prob[:, u, :, :].rearrange("p b (h j) -> p (b h) j", j=DH),
                                k.scores[:, :].rearrange("p (h j) -> p h j", j=DH),
                                row_max[:, :].unsqueeze(2).broadcast_to([P, 16, DH]),
                                ALU.subtract).then_inc(S["sub_ready"], 1)

    def act_exp(act, g, n, u):
        act.wait_ge(S["sub_ready"], g + 2)
        nc.scalar.activation(prob[:, u, :, :], prob[:, u, :, :], ACT.Exp, scale=8.0).then_inc(S["exp_ready"], 1)

    def dve_sum(dve, g, n, u):
        dve.wait_ge(S["exp_ready"], g + 1)
        ch = Chain(dve, S["sm_link"], g * 2 + 1)
        ch.link(nc.vector.tensor_reduce(row_sum[:, :], prob[:, u, :, :].rearrange("p b (h j) -> p (b h) j", j=DH), AX,
                                        ALU.add))
        dve.wait_ge(S["prob_ready"], g + 1)
        nc.vector.reciprocal(row_inv[:, u, :], row_sum[:, :]).then_inc(S["inv_ready"], 1)

    def pool_prob(pool, g, n, u):
        pool.wait_ge(S["inv_ready"], g + 1)
        pr = prob[:, u, :, :].rearrange("p b (h j) -> p (b h) j", j=DH)
        nc.gpsimd.tensor_tensor(pr, pr, row_inv[:, u, :].unsqueeze(2).broadcast_to([P, 16, DH]),
                                ALU.mult).then_inc(S["prob_ready"], 1)

    def c_bank(u, j):
        return bank[6 + (u + j) % 2]

    def pe_prob(pe, g, n, u):
        base = g * 7
        pe.wait_ge(S["prob_ready"], g + 3)
        for wb in range(2):
            pe.wait_ge(S["c_evac"], base + wb + 1)
            for m in range(4):
                ins = nc.tensor.transpose(c_bank(u, wb)[:, m * P:(m + 1) * P],
                                          prob[:, u, wb, m * P:(m + 1) * P], ident[:, :])
            ins.then_inc(S["c_done"], 1)

    def pe_attend(pe, g, n, u):
        base = g * 7
        pe.wait_ge(S["tr_evac"], g * 5 + 3)
        for j in range(4):
            hpl, wb = j // 2, j % 2
            pe.wait_ge(S["c_evac"], base + 2 + j + 1)
            for w2 in range(2):
                ins = nc.tensor.matmul(
                    c_bank(u, 2 + j)[:, w2 * 256:(w2 + 1) * 256],
                    x_keys[64 * hpl:64 * hpl + 64, u, 2 * wb + w2, :],
                    prob_t[64 * hpl:64 * hpl + 64, wb, :, 64 * w2:64 * w2 + 64], start=True, stop=True)
            ins.then_inc(S["c_done"], 1)

    def pe_out(pe, g, n, u, part):
        base = g * 7
        for i in range(4 * part, 4 * part + 4):
            if i == 0:
                pe.wait_ge(S["c_evac"], base + 7)
            if i == HP:
                pe.wait_ge(S["c_evac"], base + 8)
            hpl, hpp, h2 = i // 8, (i % 8) // 2, i % 2
            ins = nc.tensor.matmul(c_bank(u, 6)[:, 0:BLK], w_vo[:, HP * h2 + 2 * hpp + hpl, :], y_t[:, i, :],
                                   start=(i == 0), stop=(i == HEADS - 1))
        if part == 3:
            ins.then_inc(S["c_done"], 1)

    def act_prob(act, g, n, u):
        base = g * 7 + 14
        for wb in range(2):
            act.wait_ge(S["c_done"], base + wb + 1)
            nc.scalar.activation(prob_t[:, wb, :, :], c_bank(u, wb)[:, :].rearrange("p (h c) -> p h c", h=4),
                                 ACT.Copy).then_inc(S["c_evac"], 1)

    def act_attend(act, g, n, u, part):
        base = g * 7 + 14
        for j in range(2 * part, 2 * part + 2):
            hpl, wb = j // 2, j % 2
            act.wait_ge(S["c_done"], base + 2 + j + 1)
            for w2 in range(2):
                w = 2 * wb + w2
                ins = nc.scalar.activation(
                    y_t[:, 8 * hpl:8 * hpl + 8, w * WIN:(w + 1) * WIN],
                    c_bank(u, 2 + j)[:, w2 * 256:(w2 + 1) * 256].rearrange("p (h q) -> p h q", q=WIN), ACT.Copy)
            ins.then_inc(S["c_evac"], 1)

    def act_out(act, g, n, u):
        act.wait_ge(S["c_done"], g * 7 + 21)
        act.wait_ge(S["xb_ready"], g + 1)
        nc.scalar.activation(o_t[:, u, :], c_bank(u, 6)[:, 0:BLK], ACT.Copy).then_inc(S["c_evac"], 1)

    def pool_residual(pool, g, n, u):
        pool.wait_ge(S["c_evac"], g * 7 + 9)
        at = bass.ds(blk_off(n), BLK)
        nc.gpsimd.tensor_tensor(x_b[:, at], x_a[:, at], o_t[:, u, :], ALU.add).then_inc(S["xb_ready"], 1)

    STEPS = {
        "tensor": [(pe_prob, 3), (pe_project, 0), (pe_attend, 3), (pe_out, 3, 0), (pe_keys, 1), (pe_heads, 1, 0),
                   (pe_out, 3, 1), (pe_heads, 1, 1), (pe_out, 3, 2), (pe_heads, 1, 2),
                   (pe_heads, 1, 3), (pe_out, 3, 3), (pe_scores, 1)],
        "scalar": [(act_prob, 3), (act_project, 0), (act_attend, 3, 0), (act_square, 0, 2),
                   (act_square, 0, 3), (act_attend, 3, 1), (act_exp, 2), (act_scores, 1), (act_out, 3),
                   (act_norms, 0)],
        "vector": [(dve_scale, 1), (dve_max, 2), (dve_norms, 0), (dve_sum, 2), (dve_rope, 0)],
        "gpsimd": [(pool_rope, 0), (pool_shift, -1), (pool_prob, 2), (pool_residual, 3), (pool_tail, 1)],
    }

    def attention(eng, steps, layer, first_done=None, ahead={}):
        def step(m, u, low, high, order):
            for f, lag, *part in order:
                if low <= lag <= high:
                    if isinstance(m, int) and (m, f, *part) in ahead:
                        ahead[(m, f, *part)]()
                    f(eng, layer * NBLK + (m - lag), m - lag, (u - lag) % 2, *part)

        early = [s for s in steps if s[1] < 0]
        if early:
            step(-1, 1, -1, -1, early)
        step(0, 0, -1, 0, early + [s for s in steps if s[1] >= 0 and s[0] is not act_norms])
        if first_done:
            eng.wait_ge(*first_done)
        for m in range(1, 4):
            step(m, m % 2, -1, m, steps)
        with eng.Fori(2, NBLK // 2 - 1) as pair:
            for u in range(2):
                step(pair * 2 + u, u, -1, 3, steps)
        for m in range(NBLK - 2, NBLK + 3):
            step(m, m % 2, m - NBLK + 1, 3, steps)


    def pool_ffn_shift(pool, q, c, u):
        pool.wait_ge(S["f_cen"], q + 1)
        ch = Chain(pool, S["f_shift_link"], q)
        k.settle(pool)
        ch.link(nc.gpsimd.tensor_copy(xf[0:64, u, :], x_b[0:64, bass.ds(chunk_off(c), CH)]))
        k.settle(pool)
        nc.gpsimd.tensor_copy(xf[64:128, u, :], x_b[64:128, bass.ds(chunk_off(c) - 1, CH)]).then_inc(S["f_xs"], 1)
        pool.wait_ge(S["f_xs"], q + 1)
        k.settle(pool)

    def pe_ffn_centre(pe, q, c, u):
        pe.wait_ge(S["f_xs"], q + 1)
        pe.wait_ge(S["f_xn"], q + 1)
        nc.tensor.matmul(bank[0][:, :], k.centre[:, :], xf[:, u, :], start=True, stop=True).then_inc(S["f_cen"], 1)

    def pe_ffn_var(pe, q, c, u):
        pe.wait_ge(S["f_sq"], q + 1)
        variance(nc, k, bank[1], f_sq).then_inc(S["f_var"], 1)

    def pe_ffn_spread(pe, q, c, u):
        pe.wait_ge(S["f_inv"], q + 2)
        spread_inverse(nc, k, bank[1], 0).then_inc(S["f_bc"], 1)

    def pe_ffn_up(pe, q, c, u, part):
        pe.wait_ge(S["f_xn"], q + 2)
        for j, (r, m) in list(enumerate(FIT))[part:part + 1]:
            pe.wait_ge(S["f_gate"], q * 3 + j + 1)
            nc.tensor.matmul(bank[2 + (u + j) % 2][0:m, :], w1[:, FI + r:FI + r + m], xn[:, u, :],
                             start=True, stop=True).then_inc(S["f_gate_mm"], 1)
            pe.wait_ge(S["f_hid"], q * 3 + j + 1)
            nc.tensor.matmul(bank[4 + (u + j) % 2][0:m, :], w1[:, r:r + m], xn[:, u, :],
                             start=True, stop=True).then_inc(S["f_a_mm"], 1)

    def pe_ffn_down(pe, q, c, u):
        pe.wait_ge(S["xa_ready"], q + 1)
        for j, (r, m) in enumerate(FIT):
            pe.wait_ge(S["f_hid"], q * 3 + j + 3)
            ins = nc.tensor.matmul(bank[6 + u][:, :], w2[0:m, j, :], hid[0:m, j, :], start=(j == 0), stop=(j == 2))
        ins.then_inc(S["f_out_mm"], 1)

    def act_ffn_square(act, q, c, u):
        act.wait_ge(S["f_cen"], q + 3)
        act.wait_ge(S["f_var"], q + 1)
        nc.scalar.activation(f_sq, bank[0][:, :], ACT.Square).then_inc(S["f_sq"], 1)
        nc.scalar.activation(f_cen, bank[0][:, :], ACT.Copy).then_inc(S["f_copy"], 1)

    def act_ffn_gate(act, q, c, u, part):
        for j, (r, m) in list(enumerate(FIT))[part:part + 1]:
            act.wait_ge(S["f_gate_mm"], q * 3 + j + 1)
            act.wait_ge(S["f_hid"], q * 3 + j + 1)
            nc.scalar.activation(gate[0:m, (u + j) % 2, :], bank[2 + (u + j) % 2][0:m, :], ACT.Gelu,
                                 bias=fvec[0:m, 6 + j:7 + j]).then_inc(S["f_gate"], 1)

    def act_ffn_std(act, q, c, u):
        act.wait_ge(S["f_var"], q + 2)
        act.wait_ge(S["f_inv"], q + 1)
        nc.scalar.activation(k.nstd[:, :], bank[1][:, 0:QPC], ACT.Sqrt, bias=k.eps[:, 0:1]).then_inc(S["f_std"], 1)

    def dve_ffn_hidden(dve, q, c, u, part):
        if part == 0:
            dve.wait_ge(S["f_out_mm"], q + 1)
        for j, (r, m) in list(enumerate(FIT))[part:part + 1]:
            dve.wait_ge(S["f_gate"], q * 3 + j + 3)
            dve.wait_ge(S["f_a_mm"], q * 3 + j + 1)
            nc.vector.scalar_tensor_tensor(out=hid[0:m, j, :], in0=bank[4 + (u + j) % 2][0:m, :],
                                           scalar=fvec[0:m, 3 + j:4 + j], in1=gate[0:m, (u + j) % 2, :],
                                           op0=ALU.add, op1=ALU.mult).then_inc(S["f_hid"], 1)

    def dve_ffn_inverse(dve, q, c, u):
        dve.wait_ge(S["f_std"], q + 1)
        dve.wait_ge(S["f_bc"], q + 1)
        nc.vector.reciprocal(k.ninv[:, 0, :], k.nstd[:, :]).then_inc(S["f_inv"], 1)

    def dve_ffn_norm(dve, q, c, u):
        dve.wait_ge(S["f_bc"], q + 2)
        dve.wait_ge(S["f_copy"], q + 1)
        ch = Chain(dve, S["f_link"], q)
        ch.link(nc.vector.tensor_tensor(f_tmp, bank[1][:, :], f_cen, ALU.mult))
        nc.vector.tensor_scalar(xn[:, u, :], f_tmp, fvec[:, 0:1], fvec[:, 1:2], ALU.mult,
                                ALU.add).then_inc(S["f_xn"], 1)

    def dve_ffn_out(dve, q, c, u):
        dve.wait_ge(S["f_out_mm"], q + 2)
        at = bass.ds(chunk_off(c), CH)
        nc.vector.scalar_tensor_tensor(out=x_a[:, at], in0=bank[6 + u][:, :], scalar=fvec[:, 2:3], in1=x_b[:, at],
                                       op0=ALU.add, op1=ALU.add).then_inc(S["xa_ready"], 1)

    FSTEPS = {
        "tensor": [(pe_ffn_centre, -1), (pe_ffn_up, 0, 0), (pe_ffn_var, -1), (pe_ffn_up, 0, 1), (pe_ffn_spread, -1),
                   (pe_ffn_up, 0, 2), (pe_ffn_down, 0)],
        "scalar": [(act_ffn_square, -1), (act_ffn_gate, 0, 0), (act_ffn_std, -1), (act_ffn_gate, 0, 1),
                   (act_ffn_gate, 0, 2)],
        "vector": [(dve_ffn_hidden, 0, 0), (dve_ffn_inverse, -1), (dve_ffn_hidden, 0, 1), (dve_ffn_norm, -1),
                   (dve_ffn_hidden, 0, 2), (dve_ffn_out, 0)],
        "gpsimd": [(pool_ffn_shift, -2)],
    }

    def ffn_step(eng, steps, layer, m, u, low, high):
        for f, lag, *part in steps:
            if low <= lag <= high:
                f(eng, layer * NCH + (m - lag), m - lag, (u - lag) % 2, *part)

    def ffn(eng, steps, layer):
        k.settle(eng)
        with eng.Fori(0, NCH // 2 - 1) as pair:
            for u in range(2):
                ffn_step(eng, steps, layer, pair * 2 + u, u, -2, 0)
        ffn_step(eng, steps, layer, NCH - 2, 0, -1, 0)
        ffn_step(eng, steps, layer, NCH - 1, 1, 0, 0)


    def sync(sp):
        sp.dma_start(k.mask_by_block[:, :].bitcast(U16), dram["mask_tab"]).then_inc(S["const_loaded"], 16)
        sp.dma_start(ident_bf[:, :].bitcast(U16), dram["ident_bf"]).then_inc(S["const_loaded"], 16)

        def load(layer):
            sp.dma_start(w_qk[:, :], dram["w_qk"][bass.ds(layer * P, P), :]).then_inc(S["qk_loaded"], 16)

        def load_vo(layer):
            sp.dma_start(wv_t[:, :, :], dram["wv_t"][bass.ds(layer * P, P), :, :]).then_inc(S["vo_loaded"], 16)
            sp.dma_start(w_o[:, :, :], dram["w_o"][bass.ds(layer * P, P), :, :]).then_inc(S["vo_loaded"], 16)

        def load_scale(layer):
            sp.dma_start(rot[:, :, :], dram["rot_tab"]).then_inc(S["scale_loaded"], 16)
            sp.dma_start(rot_scale[:, :], dram["rot_scale"][bass.ds(layer, 1), :].broadcast_to([P, 256])
                         ).then_inc(S["scale_loaded"], 16)

        def load_ffn(layer):
            sp.dma_start(w1[:, :], dram["w1"][bass.ds(layer * P, P), :]).then_inc(S["ffn_loaded"], 16)
            sp.dma_start(w2[:, :, :], dram["w2"][bass.ds(layer * P, P), :, :]).then_inc(S["ffn_loaded"], 16)
            sp.dma_start(fvec[:, :], dram["fvec"][bass.ds(layer * P, P), :]).then_inc(S["ffn_loaded"], 16)

        load_vo(0)
        load_scale(0)
        load(0)
        load_ffn(0)
        with sp.Fori(0, DEPTH - 1) as layer:
            sp.wait_ge(S["vo_done"], layer * 4 + 4)
            load_vo(layer + 1)
            sp.wait_ge(S["proj_done"], layer * 4 * NBLK + 4 * NBLK)
            load(layer + 1)
            sp.wait_ge(S["rope_ready"], layer * NBLK + NBLK + 2)
            load_scale(layer + 1)
            sp.wait_ge(S["xa_ready"], layer * NCH + NCH + 2)
            load_ffn(layer + 1)

    FFN_DMAS = 3

    def tensor(pe):
        pe.sem_inc(S["tr_done"], 10)
        pe.sem_inc(S["c_done"], 14)
        pe.sem_inc(S["sim_done"], 2)
        pe.sem_inc(S["f_cen"], 2)
        pe.sem_inc(S["f_var"], 1)
        pe.sem_inc(S["f_bc"], 1)
        pe.sem_inc(S["f_out_mm"], 1)
        pe.wait_ge(k.N["n_out"], (norm_index + 1) * NCH + 2)
        pe.wait_ge(S["const_loaded"], 32)
        with pe.Fori(0, DEPTH) as layer:
            pe.wait_ge(S["vo_loaded"], layer * 32 + 32)
            pe.wait_ge(S["xa_ready"], layer * NCH + 2)
            for j in range(4):
                for m in range(4):
                    r, hp = 64 * (j // 2), 4 * (j % 2) + m
                    ins = nc.tensor.matmul(bank[j][:, m * D:(m + 1) * D], wv_t[r:r + 64, hp, :],
                                           w_o[r:r + 64, hp, :], start=True, stop=True)
                ins.then_inc(S["vo_done"], 1)
            pe.wait_ge(S["vo_evac"], layer * 4 + 4)
            pe.wait_ge(S["qk_loaded"], layer * 16 + 16)

            def centre():
                pe.wait_ge(S["proj_evac"], layer * 4 * NBLK + 4 * NBLK + 2)
                pe_ffn_centre(pe, layer * NCH, 0, 0)

            attention(pe, STEPS["tensor"], layer, ahead={
                (NBLK + 2, pe_prob): centre, (NBLK + 2, pe_attend): lambda: pe_ffn_var(pe, layer * NCH, 0, 0),
                (NBLK + 2, pe_out, 3): lambda: pe_ffn_spread(pe, layer * NCH, 0, 0)})
            pe.wait_ge(S["ffn_loaded"], layer * 16 * FFN_DMAS + 16 * FFN_DMAS)
            pe.wait_ge(S["c_evac"], layer * 7 * NBLK + 7 * NBLK + 2)
            ffn(pe, FSTEPS["tensor"], layer)

    def scalar(act):
        act.sem_inc(S["proj_evac"], 2)
        act.sem_inc(S["rn_ready"], 1)
        act.sem_inc(S["tr_evac"], 2)
        act.sem_inc(S["c_evac"], 2)
        act.sem_inc(S["f_gate"], 2)
        act.wait_ge(S["layer_init"], 4)
        with act.Fori(0, DEPTH) as layer:
            for j in range(4):
                act.wait_ge(S["vo_done"], layer * 4 + j + 1)
                nc.scalar.activation(w_vo[:, 4 * j:4 * j + 4, :], bank[j][:, :].rearrange("p (h d) -> p h d", h=4),
                                     ACT.Copy).then_inc(S["vo_evac"], 1)

            def square():
                act.wait_ge(S["sq_summed"], layer * NBLK + NBLK + 1)
                act_ffn_square(act, layer * NCH, 0, 0)

            attention(act, STEPS["scalar"], layer, ahead={
                (1, act_scores): lambda: act_norms(act, layer * NBLK, 0, 0),
                (NBLK + 2, act_prob): square, (NBLK + 2, act_out): lambda: act_ffn_std(act, layer * NCH, 0, 0)})
            act.wait_ge(S["ffn_loaded"], layer * 16 * FFN_DMAS + 16 * FFN_DMAS)
            ffn(act, FSTEPS["scalar"], layer)

    def vector(dve):
        dve.sem_inc(S["sq_summed"], 1)
        dve.sem_inc(S["rot_link"], 3)
        dve.sem_inc(S["rope_ready"], 2)
        dve.sem_inc(S["sub_ready"], 1)
        dve.sem_inc(S["f_xn"], 1)
        dve.sem_inc(S["f_inv"], 1)
        dve.sem_inc(S["f_hid"], 2)
        dve.sem_inc(S["xa_ready"], 2)
        with dve.Fori(0, DEPTH) as layer:
            dve.wait_ge(S["rot_ready"], layer + 1)

            attention(dve, STEPS["vector"], layer)
            dve.wait_ge(S["ffn_loaded"], layer * 16 * FFN_DMAS + 16 * FFN_DMAS)
            ffn_step(dve, FSTEPS["vector"], layer, -1, 1, -1, -1)
            dve.wait_ge(S["xb_ready"], layer * NBLK + NBLK + 2)
            ffn(dve, FSTEPS["vector"], layer)

    def gpsimd(pool):
        nc.gpsimd.memset(k.has_next[:, 0:BPS - 1], 1.0).then_inc(S["layer_init"], 1)
        nc.gpsimd.memset(k.has_next[:, BPS - 1:BPS], 0.0).then_inc(S["layer_init"], 1)
        pool.sem_inc(S["tail_ready"], 1)
        pool.sem_inc(S["prob_ready"], 2)
        pool.sem_inc(S["xb_ready"], 2)
        nc.gpsimd.memset(k_t[:, 0, :, 0:WIN], 0.0).then_inc(S["layer_init"], 1)
        nc.gpsimd.memset(q_z[:, :, :, :, :, :], 0.0).then_inc(S["layer_init"], 1)
        pool.wait_ge(S["layer_init"], 4)
        pool.wait_ge(k.N["n_out"], (norm_index + 1) * NCH + 2)
        pool.wait_ge(S["const_loaded"], 32)
        with pool.Fori(0, DEPTH) as layer:
            pool.wait_ge(S["scale_loaded"], layer * 32 + 32)
            nc.gpsimd.tensor_tensor(rot[:, :, :], rot[:, :, :],
                                    rot_scale[:, :].unsqueeze(1).broadcast_to([P, BPS, 256]),
                                    ALU.mult).then_inc(S["rot_ready"], 1)
            pool.wait_ge(S["rot_ready"], layer + 1)

            def shift():
                pool.wait_ge(S["xb_ready"], layer * NBLK + 2 * (NBLK // NCH) + 2)
                pool.wait_ge(S["tr_done"], (layer * NBLK + NBLK) * 5 + 10)
                k.settle(pool)
                for c in range(2):
                    pool_ffn_shift(pool, layer * NCH + c, c, c)

            attention(pool, STEPS["gpsimd"], layer, first_done=(S["xa_ready"], layer * NCH + 2), ahead={(NBLK + 1, pool_prob): shift})
            pool.wait_ge(S["xb_ready"], layer * NBLK + NBLK + 2)
            k.settle(pool)
            ffn(pool, FSTEPS["gpsimd"], layer)
            pool.wait_ge(S["xa_ready"], layer * NCH + 3)

    k.layers_done = (S["xa_ready"], DEPTH * NCH + 2)
    return {"sync": sync, "tensor": tensor, "scalar": scalar, "vector": vector, "gpsimd": gpsimd}

def after(k, part, done):
    def waiting(program):
        def run(eng):
            if done:
                eng.wait_ge(*done)
            program(eng)
        return run

    return {name: waiting(program) for name, program in part.items()}


def early_stages(nc, k, dram, stages):
    parts, n, last = [], 0, None
    for name, stage in (("A", ssm_stage), ("B", moe_stage), ("C", conv_stage)):
        if name not in stages:
            continue
        with ExitStack() as k.stage:
            parts.append(norm_pass(nc, k, n, k.x_in, k.x_a))
            k.norm_index = n
            parts.append(after(k, stage(nc, k, dram), last))
            last = k.stage_done
            parts.append(norm_pass(nc, k, n + 1, k.x_b, k.x_in, res=k.x_in, ready=k.stage_done))
        n += 2
    return parts, n



def build(nc, dram, out, stages="ABCD"):
    ctx = ExitStack()
    with ctx:
        k = Parts(nc, ctx)
        k.norm_links = 0
        k.stage_done = None
        k.ident = k.sb("ident", [P, P])
        k.centre = k.sb("centre", [P, P])
        k.mean = k.sb("mean", [P, P])
        k.eps = k.sb("eps", [P, 1])
        k.x_in = k.sb("x_in", [P, XW])
        k.x_a = k.sb("x_a", [P, XW])
        k.x_b = k.sb("x_b", [P, XW])
        psum = ctx.enter_context(nc.psum_tensor("banks", [P, 8 * CH], F32))
        k.bank = [psum[:, i * CH:(i + 1) * CH] for i in range(8)]
        k.bank_bf = [b.bitcast(BF16) for b in k.bank]
        k.scores = psum[:, 4 * CH:6 * CH]
        norm_parts(nc, k)
        G = k.sems("shared_loaded input_loaded zeros_made stored settled")
        k.settle = lambda eng: eng.sem_inc(G["settled"], 1)
        x_in, x_a, x_b = k.x_in, k.x_a, k.x_b

        parts = []
        npass = 0
        consts = (G["shared_loaded"], 64)
        if "A" in stages or "B" in stages or "C" in stages:
            parts, npass = early_stages(nc, k, dram, stages)
        if "D" in stages:
            with ExitStack() as k.stage:
                first = norm_pass(nc, k, npass, x_in, x_a, ready=(G["input_loaded"], 16 * NSEQ) if npass == 0 else None)
                k.has_next = k.sb("has_next", [P, BPS])
                k.mask_by_block = k.sb("mask_by_block", [P, BPS // 2 * CH], BF16)
                layers = after(k, layers_stage(nc, k, dram, npass), k.stage_done)
                last = norm_pass(nc, k, npass + 1, x_a, x_in, res=x_in, ready=k.layers_done)
                parts += [first, layers, last]
            npass += 2
        presets = norm_presets(nc, k)
        block = ctx.enter_context(nc.Block())

        def run(eng, name):
            for s, v in presets.get(name, []):
                eng.sem_inc(s, v)
            eng.wait_ge(*consts)
            eng.wait_ge(G["input_loaded"], 16 * NSEQ)
            eng.wait_ge(G["zeros_made"], 4)
            for part in parts:
                if name in part:
                    part[name](eng)

        @block.sync
        def _(sp):
            for dst, src in ((k.ident, "ident"), (k.centre, "centre"), (k.mean, "mean"), (k.eps, "eps")):
                sp.dma_start(dst[:, :], dram[src]).then_inc(G["shared_loaded"], 16)
            for s in range(NSEQ):
                at = s * SEQW + PAD
                sp.dma_start(x_in[:, at:at + SLEN], dram["x"][:, s * SLEN:(s + 1) * SLEN]
                             ).then_inc(G["input_loaded"], 16)
            for part in parts:
                if "sync" in part:
                    part["sync"](sp)
            sp.wait_ge(k.N["n_out"], npass * NCH + 2)
            for s in range(NSEQ):
                at = s * SEQW + PAD
                sp.dma_start(out[:, s * SLEN:(s + 1) * SLEN], x_in[:, at:at + SLEN]).then_inc(G["stored"], 16)
            sp.wait_ge(G["stored"], 16 * NSEQ)

        @block.tensor
        def _(pe):
            run(pe, "tensor")

        @block.scalar
        def _(act):
            run(act, "scalar")

        @block.vector
        def _(dve):
            for x in (x_a, x_b):
                for s in range(2):
                    nc.vector.memset(x[:, :].rearrange("p (s c) -> p s c", s=NSEQ)[:, 2 * s:2 * s + 2, 0:PAD],
                                     0.0).then_inc(G["zeros_made"], 1)
            run(dve, "vector")

        @block.gpsimd
        def _(pool):
            run(pool, "gpsimd")


def constants():
    import numpy as np
    f = np.float32
    half = np.arange(0, DH, 2, dtype=f)
    inv_freq = (1.0 / f(10000.0) ** (half / DH)).astype(f)
    t = np.arange(SLEN, dtype=f)
    freqs = t[:, None] * inv_freq[None, :]
    freqs = np.concatenate([freqs, freqs], -1).astype(f)
    base = ((half + f(0.4 * DH)) / f(1.4 * DH)).astype(f)
    power = (t - SLEN // 2) / f(WIN // 2)
    scale = (base[None, :] ** power[:, None]).astype(f)
    scale = np.concatenate([scale, scale], -1)
    inv = f(1.0) / scale
    sign = np.concatenate([-np.ones(DH // 2, f), np.ones(DH // 2, f)])
    rows = np.concatenate([np.cos(freqs) * scale, np.cos(freqs) * inv, np.sin(freqs) * scale * sign,
                           np.sin(freqs) * inv * sign], -1).astype(f)
    rot_tab = rows.reshape(BPS, BLK, 256).transpose(1, 0, 2)
    w2, h2, q, j = np.meshgrid(np.arange(2), np.arange(2), np.arange(WIN), np.arange(2 * WIN), indexing="ij")
    usual = np.where((q <= j) & (j <= q + WIN), 0.0, MASKED).reshape(P, 2 * WIN)
    first = np.where((q <= j) & (j <= q + WIN) & ((w2 == 1) | (j >= WIN)), 0.0, MASKED).reshape(P, 2 * WIN)
    usual, first = (np.tile(m, (1, HP)) for m in (usual, first))

    def bf16(a):
        return (np.ascontiguousarray(a, f).view(np.uint32) >> 16).astype(np.uint16)

    pick = np.zeros((3, 2 * N_ST, 2 * N_ST, P), f)
    pick[:, np.arange(2 * N_ST), np.arange(2 * N_ST), :] = 1
    spread = np.zeros((3, 2, HEADS, 2, HEADS, D // HEADS), f)
    for i in range(2):
        for hd in range(HEADS):
            spread[:, i, hd, i, hd, :] = 1
    spread = spread.reshape(96, 2, P)
    pick8 = pick[:, :EXPERTS, :EXPERTS].reshape(3 * EXPERTS, EXPERTS, P)
    pick = pick.reshape(96, 2 * N_ST, P)
    return {
        "ident": np.eye(P, dtype=f), "centre": (np.eye(P) - 1.0 / P).astype(f),
        "mean": np.full((P, P), 1.0 / P, f), "eps": np.full((P, 1), EPS, f),
        "rot_tab": np.ascontiguousarray(rot_tab), "ident_bf": bf16(np.eye(P)),
        "pick": bf16(pick), "spread": bf16(spread), "pick8": bf16(pick8),
        "rank": np.ascontiguousarray(np.broadcast_to(EXPERTS - np.arange(EXPERTS, dtype=f), (P, TB, EXPERTS))),
        "mask_tab": bf16(np.concatenate([first] + [usual] * (BPS // 2 - 1), 1)),
    }


def layouts(a):
    import numpy as np
    c = np.ascontiguousarray
    w = a["L1_ffn_Wqkv"]
    wv = w[:, :, 2 * INNER:].reshape(DEPTH, D, HP, 2 * DH)
    qs, ks = a["L1_ffn_q_scale"], a["L1_ffn_k_scale"]
    r = DH // 2
    tail = 3 * P - FI
    w2 = np.pad(a["L1_ffn_W2"], ((0, 0), (0, tail), (0, 0)))
    b1 = np.pad(a["L1_ffn_b1"].reshape(DEPTH, 2, FI), ((0, 0), (0, 0), (0, tail))).reshape(DEPTH, 6, P)
    w_x = a["L0_attn_W_x"]
    bc = w_x[DT_RANK:].T
    out = {
        "wx_dt": c(w_x[:DT_RANK].T), "wx_bc": c(np.concatenate([bc, bc, bc], 1)), "w_dt": c(a["L0_attn_W_dt"].T),
        "avec": c(np.concatenate([a["L0_attn_A_log"], a["L0_attn_b_dt"][:, None], a["L0_attn_D_param"][:, None]], 1)),
        "w_router": c(a["L0_ffn_w_router"].T), "w_up": c(a["L0_ffn_w_up"].transpose(2, 0, 1)),
        "w_dn": c(a["L0_ffn_w_down"].reshape(EXPERTS, D, UT, P).transpose(3, 0, 2, 1)),
        "evec": c(np.concatenate([a["L0_ffn_b_up"].reshape(EXPERTS, UT, P), a["L0_ffn_b_down"][:, None, :]], 1)
                  .transpose(2, 0, 1)),
        "w_lin": c(a["L1_attn_w_lin"].reshape(HEADS, TAPS, D).transpose(2, 1, 0).reshape(D, TAPS * HEADS)),
        "x": c(a["L0_attn_u"].reshape(T, D).T),
        "w_qk": c(w[:, :, :2 * INNER].reshape(DEPTH * D, 2 * INNER)),
        "wv_t": c(wv.transpose(0, 3, 2, 1).reshape(DEPTH * P, HP, D)),
        "w_o": c(a["L1_ffn_Wo"].reshape(DEPTH, HP, 2 * DH, D).transpose(0, 2, 1, 3).reshape(DEPTH * P, HP, D)),
        "rot_scale": c(np.concatenate([qs, ks, np.roll(qs, r, -1), np.roll(ks, r, -1)], -1)),
        "w1": c(a["L1_ffn_W1"].reshape(DEPTH * D, 2 * FI)),
        "w2": c(w2.reshape(DEPTH, 3, P, D).transpose(0, 2, 1, 3).reshape(DEPTH * P, 3, D)),
        "fvec": c(np.stack([a["L1_ffn_ln_g"], a["L1_ffn_ln_b"], a["L1_ffn_b2"], *b1.transpose(1, 0, 2)],
                           -1).reshape(DEPTH * D, 9)),
    }
    return out


def kernel(**inputs):
    import numpy as np
    import concourse.bacc as bacc
    from concourse.bass_utils import run_bass_kernel_spmd

    arrays = {**constants(), **layouts({n: np.asarray(v) for n, v in inputs.items()})}
    nc = bacc.Bacc("TRN2", target_bir_lowering=False, num_devices=1)
    dram = {n: nc.dram_tensor("in_" + n, a.shape, mybir.dt.from_np(a.dtype), kind="ExternalInput").ap()
            for n, a in arrays.items()}
    out = nc.dram_tensor("out_t", (D, T), F32, kind="ExternalOutput").ap()
    build(nc, dram, out)
    r = run_bass_kernel_spmd(nc, [{"in_" + n: a for n, a in arrays.items()}], core_ids=[0])
    return np.ascontiguousarray(r.results[0]["out_t"].T).reshape(NSEQ, SLEN, D)
```
